# Optimizing a Trainium2 kernel written in Bass

```python
import numpy as np
import jax
import jax.numpy as jnp

def _softmax(x, axis=-1):
    return jax.nn.softmax(x, axis=axis)

def _gelu(x):
    return jax.nn.gelu(x, approximate=True)

def _silu(x):
    return jax.nn.silu(x)

def _sigmoid(x):
    return jax.nn.sigmoid(x)

def _layernorm(x, axis=-1, eps=1e-05):
    m = jnp.mean(x, axis=axis, keepdims=True)
    v = jnp.var(x, axis=axis, keepdims=True)
    return (x - m) / jnp.sqrt(v + eps)

def _scatter_add(tgt, idx, src, axis=0):
    return tgt.at[idx].add(src)

def _segment_sum(src, seg, n):
    return jax.ops.segment_sum(src, seg, n)
kernel_name = 'mk_decoder_preln_d1_seqx_r4_effb58'

def setup_inputs(seed: int=0):
    np.random.seed(seed)
    _w = jnp.asarray

    def _rec_inputs():
        import jax
        import jax.numpy as jnp
        _rk = jax.random.key(seed)
        x = -0.0003929 + 0.9999 * jax.random.normal(jax.random.fold_in(_rk, 1), (8, 256, 256), jnp.float32)
        _lenS = 256 - jax.random.randint(jax.random.fold_in(_rk, 7), (8,), 0, max(1, 256 // 4) + 1, jnp.int32)
        _lenS2 = 120 - jax.random.randint(jax.random.fold_in(_rk, 8), (8,), 0, max(1, 120 // 4) + 1, jnp.int32)
        _ctx_1024P = jax.random.normal(jax.random.fold_in(_rk, 12), (8, 16, 256), jnp.float32)
        _ctx_1024c = jax.random.dirichlet(jax.random.fold_in(_rk, 512), 0.3 * jnp.ones((16,), jnp.float32), (8, 120))
        _ctx_1024t = jnp.einsum('bsk,bkd->bsd', _ctx_1024c, _ctx_1024P)
        _ctx_1024t = _ctx_1024t * jax.lax.rsqrt(jnp.mean(jnp.square(_ctx_1024t)) + 1e-12) * 0.953939
        ctx_1024 = 2.81802e-05 + 1.00001 * (_ctx_1024t + 0.3 * jax.random.normal(jax.random.fold_in(_rk, 612), (8, 120, 256), jnp.float32))
        _validS = jnp.arange(256)[None, :] < _lenS[:, None]
        _validS2 = jnp.arange(120)[None, :] < _lenS2[:, None]
        _causal = jnp.tril(jnp.ones((256, 256), dtype=bool))
        mask_BxS2_bf0 = jnp.logical_not(jnp.ones((8, 120), dtype=bool))
        mask_BxS2_bk1 = jnp.broadcast_to(_validS2[:, :], (8, 120))
        return (x, ctx_1024, mask_BxS2_bf0, mask_BxS2_bk1)
    x, ctx_1024, mask_BxS2_bf0, mask_BxS2_bk1 = _rec_inputs()

    def _L0_attn_setup():
        import jax, jax.numpy as jnp
        import numpy as np
        D_MODEL = 256
        NUM_HEADS = 16
        HEAD_DIM = D_MODEL // NUM_HEADS
        key = jax.random.key(seed)
        ks = jax.random.split(key, 9)
        B, S = (4, 512)
        scale = 1.0 / np.sqrt(D_MODEL)
        x = jax.random.normal(ks[0], (B, S, D_MODEL), dtype=jnp.float32)
        Wq = jax.random.normal(ks[1], (D_MODEL, D_MODEL), dtype=jnp.float32) * scale
        bq = jnp.zeros((D_MODEL,), dtype=jnp.float32)
        Wk = jax.random.normal(ks[2], (D_MODEL, D_MODEL), dtype=jnp.float32) * scale
        bk = jnp.zeros((D_MODEL,), dtype=jnp.float32)
        Wv = jax.random.normal(ks[3], (D_MODEL, D_MODEL), dtype=jnp.float32) * scale
        bv = jnp.zeros((D_MODEL,), dtype=jnp.float32)
        Wo = jax.random.normal(ks[4], (D_MODEL, D_MODEL), dtype=jnp.float32) * scale
        bo = jnp.zeros((D_MODEL,), dtype=jnp.float32)
        return {'x': x, 'Wq': Wq, 'bq': bq, 'Wk': Wk, 'bk': bk, 'Wv': Wv, 'bv': bv, 'Wo': Wo, 'bo': bo}
    _L0_attn_all = _L0_attn_setup()
    _L0_attn_in = {k: v for k, v in _L0_attn_all.items() if k in ('Wq', 'bq', 'Wk', 'bk', 'Wv', 'bv', 'Wo', 'bo')}
    del _L0_attn_all

    def _L0_xattn_setup():
        import jax, jax.numpy as jnp
        import numpy as np
        key = jax.random.key(seed)
        ks = jax.random.split(key, 6)
        B, P, Q, D_IN, D_H = (8, 512, 512, 256, 256)
        passage = jax.random.normal(ks[0], (B, P, D_IN), dtype=jnp.float32)
        question = jax.random.normal(ks[1], (B, Q, D_IN), dtype=jnp.float32)
        rep = jax.random.normal(ks[2], (B, Q, D_H), dtype=jnp.float32)
        p_mask = jnp.zeros((B, P), dtype=bool)
        q_mask = jax.random.randint(ks[3], (B, Q), 0, 2).astype(bool)
        limit = np.sqrt(6.0 / (D_IN + D_H))
        U_w = jax.random.uniform(ks[4], (D_H, D_IN), dtype=jnp.float32, minval=-limit, maxval=limit)
        D_param = jnp.ones((1, D_H), dtype=jnp.float32)
        return {'passage': passage, 'p_mask': p_mask, 'question': question, 'q_mask': q_mask, 'rep': rep, 'U_w': U_w, 'D_param': D_param}
    _L0_xattn_all = _L0_xattn_setup()
    _L0_xattn_in = {k: v for k, v in _L0_xattn_all.items() if k in ('U_w', 'D_param')}
    del _L0_xattn_all

    def _L0_ffn_setup():
        import jax, jax.numpy as jnp
        import numpy as np
        D_MODEL, D_FF, RANK = (256, 1024, 64)
        B, S = (4, 1024)
        key = jax.random.key(seed)
        ks = jax.random.split(key, 7)
        return {'x': jax.random.normal(ks[0], (B, S, D_MODEL), dtype=jnp.float32), 'U1': jax.random.normal(ks[1], (D_MODEL, RANK), dtype=jnp.float32) * 0.02, 'V1': jax.random.normal(ks[2], (RANK, D_FF), dtype=jnp.float32) * 0.02, 'b1': jnp.zeros((D_FF,), dtype=jnp.float32), 'U2': jax.random.normal(ks[3], (D_FF, RANK), dtype=jnp.float32) * 0.02, 'V2': jax.random.normal(ks[4], (RANK, D_MODEL), dtype=jnp.float32) * 0.02, 'b2': jnp.zeros((D_MODEL,), dtype=jnp.float32)}
    _L0_ffn_all = _L0_ffn_setup()
    _L0_ffn_in = {k: v for k, v in _L0_ffn_all.items() if k in ('U1', 'V1', 'b1', 'U2', 'V2', 'b2')}
    del _L0_ffn_all
    return {'x': x, 'ctx_1024': ctx_1024, 'mask_BxS2_bf0': mask_BxS2_bf0, 'mask_BxS2_bk1': mask_BxS2_bk1, 'L0_attn_Wq': _L0_attn_in['Wq'], 'L0_attn_bq': _L0_attn_in['bq'], 'L0_attn_Wk': _L0_attn_in['Wk'], 'L0_attn_bk': _L0_attn_in['bk'], 'L0_attn_Wv': _L0_attn_in['Wv'], 'L0_attn_bv': _L0_attn_in['bv'], 'L0_attn_Wo': _L0_attn_in['Wo'], 'L0_attn_bo': _L0_attn_in['bo'], 'L0_xattn_U_w': _L0_xattn_in['U_w'], 'L0_xattn_D_param': _L0_xattn_in['D_param'], 'L0_ffn_U1': _L0_ffn_in['U1'], 'L0_ffn_V1': _L0_ffn_in['V1'], 'L0_ffn_b1': _L0_ffn_in['b1'], 'L0_ffn_U2': _L0_ffn_in['U2'], 'L0_ffn_V2': _L0_ffn_in['V2'], 'L0_ffn_b2': _L0_ffn_in['b2']}

def reference(x, ctx_1024, mask_BxS2_bf0, mask_BxS2_bk1, L0_attn_Wq, L0_attn_bq, L0_attn_Wk, L0_attn_bk, L0_attn_Wv, L0_attn_bv, L0_attn_Wo, L0_attn_bo, L0_xattn_U_w, L0_xattn_D_param, L0_ffn_U1, L0_ffn_V1, L0_ffn_b1, L0_ffn_U2, L0_ffn_V2, L0_ffn_b2):
    import jax
    import jax.numpy as jnp

    def _L0_attn_ref(x, Wq, bq, Wk, bk, Wv, bv, Wo, bo):
        import jax, jax.numpy as jnp
        import numpy as np
        D_MODEL = 256
        NUM_HEADS = 16
        HEAD_DIM = D_MODEL // NUM_HEADS
        B, S, _ = x.shape
        H, Dh = (NUM_HEADS, HEAD_DIM)
        q = (x @ Wq.T + bq).reshape(B, S, H, Dh).transpose(0, 2, 1, 3)
        k = (x @ Wk.T + bk).reshape(B, S, H, Dh).transpose(0, 2, 1, 3)
        v = (x @ Wv.T + bv).reshape(B, S, H, Dh).transpose(0, 2, 1, 3)
        scores = jnp.einsum('bhqd,bhkd->bhqk', q, k) / np.sqrt(Dh)
        attn = jax.nn.softmax(scores, axis=-1)
        ctx = jnp.einsum('bhqk,bhkd->bhqd', attn, v)
        ctx = ctx.transpose(0, 2, 1, 3).reshape(B, S, H * Dh)
        return ctx @ Wo.T + bo

    def _L0_xattn_ref(passage, p_mask, question, q_mask, rep, U_w, D_param):
        import jax, jax.numpy as jnp
        import numpy as np
        Up = jax.nn.relu(jnp.einsum('bpi,hi->bph', passage, U_w))
        Uq = jax.nn.relu(jnp.einsum('bqi,hi->bqh', question, U_w))
        Uq = D_param[0] * Uq
        scores = jnp.einsum('bph,bqh->bpq', Up, Uq)
        scores = jnp.where(q_mask[:, None, :], -jnp.inf, scores)
        alpha = jax.nn.softmax(scores, axis=2)
        return jnp.einsum('bpq,bqh->bph', alpha, rep)

    def _L0_ffn_ref(x, U1, V1, b1, U2, V2, b2):
        import jax, jax.numpy as jnp
        import numpy as np
        D_MODEL, D_FF, RANK = (256, 1024, 64)
        B, S = (4, 1024)
        P = jnp.einsum('bsd,dr->bsr', x, U1)
        H = jax.nn.gelu(jnp.einsum('bsr,rf->bsf', P, V1) + b1)
        Q = jnp.einsum('bsf,fr->bsr', H, U2)
        return jnp.einsum('bsr,rd->bsd', Q, V2) + b2
    x = x + _L0_attn_ref(_layernorm(x, axis=-1), L0_attn_Wq, L0_attn_bq, L0_attn_Wk, L0_attn_bk, L0_attn_Wv, L0_attn_bv, L0_attn_Wo, L0_attn_bo)
    x = x + _L0_xattn_ref(_layernorm(x, axis=-1), mask_BxS2_bf0, ctx_1024, mask_BxS2_bk1, ctx_1024, L0_xattn_U_w, L0_xattn_D_param)
    x = x + _L0_ffn_ref(_layernorm(x, axis=-1), L0_ffn_U1, L0_ffn_V1, L0_ffn_b1, L0_ffn_U2, L0_ffn_V2, L0_ffn_b2)
    return x

_drawn_inputs = setup_inputs


def setup_inputs(seed=0):
    import zlib

    import numpy as np

    out = dict(_drawn_inputs(seed))
    spreads = {'L0_attn_bq': (0.0, 0.528),
     'L0_attn_bk': (0.0, 2.0),
     'L0_attn_bv': (0.0, 0.1),
     'L0_attn_bo': (0.0, 0.1),
     'L0_xattn_D_param': (1.0, 0.2),
     'L0_ffn_b1': (0.0, 0.8),
     'L0_ffn_b2': (0.0, 0.8)}
    factors = {'L0_ffn_U1': 8.0, 'L0_ffn_V1': 8.0, 'L0_ffn_U2': 8.0, 'L0_ffn_V2': 8.0}
    for name, (base, spread) in spreads.items():
        noise = np.random.default_rng([zlib.crc32(name.encode()), seed]).standard_normal(out[name].shape)
        drawn = base * np.exp(spread * noise) if base else spread * noise
        out[name] = jnp.asarray(drawn.astype(out[name].dtype))
    for name, factor in factors.items():
        out[name] = (out[name] * factor).astype(out[name].dtype)
    return out
```

```python
from contextlib import ExitStack

import numpy as np
import concourse.bass as bass
from concourse import mybir

ALU = mybir.AluOpType
ACT = mybir.ActivationFunctionType
AX = mybir.AxisListType
F32 = mybir.dt.float32
F32R = mybir.dt.float32r
BF16 = mybir.dt.bfloat16
U8 = mybir.dt.uint8

P = 128
EPS = 1e-5
MASKED = -3.0e38
Q_PARTS = (0, 0, 0, 1, 1, 2)
K_PARTS = (0, 1, 2, 0, 1, 0)


class Batch:

    def __init__(self, b, parity, turn):
        self.b, self.parity, self.turn = b, parity, turn


def batch_at(pair, k):
    return Batch(2 * pair + k, k % 2, pair + k // 2)


def decoder_layer(nc, io):
    B, S, D = io["x"].shape
    SC = io["ctx"].shape[1]
    NT, NC = S // P, D // P
    H, DH = 16, D // 16
    HC = H // NC
    HG = 4
    NG = H // HG
    W = 32
    F = io["b1"].shape[0] * io["b1"].shape[1]
    NF = F // P
    R = io["u1"].shape[-1]
    NP = len(Q_PARTS)
    KR = NP * DH
    KM = KR + 3
    SCALE = float(DH) ** -0.5
    FT = 2 * NT
    FN = FT * P
    W_LOADS = 20
    assert S == 2 * P and D == 2 * P and R == 64 and H % HG == 0 and B % 2 == 0

    ctx = ExitStack()
    with ctx:
        def sb(name, shape, dt=F32):
            return ctx.enter_context(nc.sbuf_tensor(name, shape, dt))

        def sem(name):
            return ctx.enter_context(nc.semaphore(name))

        ident = sb("ident", [P, P])
        ident_bf = sb("ident_bf", [P, P], BF16)
        weights = {}
        for n, cols in (("wq", D), ("wk", D), ("wv", D), ("wo", D), ("uw", D), ("u1", P)):
            weights[n] = (sb(n + "_f", [P, NC, cols]), sb(n + "_h", [P, NC, cols], F32R), sb(n + "_l", [P, NC, cols], F32R))
        weights["v1"] = (sb("v1_f", [P, F]), sb("v1_h", [P, F], F32R), sb("v1_l", [P, F], F32R))
        u2 = sb("u2", [P, NF, R])
        v2 = sb("v2", [P, D])
        bq, bk, dpar = sb("bq_sb", [P, NC]), sb("bk_sb", [P, NC]), sb("dpar_sb", [P, NC])
        b1 = sb("b1_sb", [P, NF])
        bv, bo, b2 = sb("bv_sb", [P, D]), sb("bo_sb", [P, D]), sb("b2_sb", [P, D])
        mask_u8 = sb("mask_u8", [P, B, SC], U8)
        neg_mask = sb("neg_mask", [P, SC])
        wait_pad = sb("wait_pad", [P, 1])
        minus_half, eps_sb = sb("minus_half", [P, FT]), sb("eps", [P, FT])

        xres = sb("xres", [P, B, NT, D])
        cbuf = [sb(f"cbuf{i}", [SC, D]) for i in range(2)]
        stats = [sb(f"stats{i}", [P, FT, 6]) for i in range(3)]
        mv = [sb(f"mv{i}", [P, FT, 2]) for i in range(3)]
        var_eps = [sb(f"var_eps{i}", [P, FT]) for i in range(3)]
        rstd = [sb(f"rstd{i}", [P, FT]) for i in range(3)]
        xn = sb("xn", [P, NT, D])
        xT = (sb("xT_h", [P, NC, S], F32R), sb("xT_l", [P, NC, S], F32R))
        qf, kf = sb("qf", [P, NC, S]), sb("kf", [P, NC, S])
        qr, kr = sb("qr", [P, NC, S]), sb("kr", [P, NC, S])
        qp, kp = sb("qp", [P, 3, NC, S], BF16), sb("kp", [P, 3, NC, S], BF16)
        qs = [sb(f"qs{i}", [P, H, S], BF16) for i in range(2)]
        ks = [sb(f"ks{i}", [P, H, S], BF16) for i in range(2)]
        vsb = [sb(f"v{i}", [P, NT, H, W]) for i in range(2)]
        smax = sb("smax", [P, NT, H])
        smax_r = sb("smax_r", [P, NT, H])
        smax_p = sb("smax_p", [P, NT, 5, H], BF16)
        smax_T = sb("smax_T", [3 * H, S], BF16)
        probs = [sb(f"probs{i}", [P, HG, NT, S]) for i in range(2)]
        att_raw = sb("att_raw", [P, NG, S])
        att_rec = sb("att_rec", [P, NT, H])
        att = sb("att", [P, NT, D])
        attT = (sb("attT_h", [P, NC, S], F32R), sb("attT_l", [P, NC, S], F32R))
        x1 = sb("x1", [P, NT, D])
        x1n = sb("x1n", [P, NT, D])
        x1T = (sb("x1T_h", [P, NC, S], F32R), sb("x1T_l", [P, NC, S], F32R))
        cT = sb("cT", [P, NC, SC])
        upT = sb("upT", [P, NC, S])
        uqT = sb("uqT", [P, NC, SC])
        xsc = sb("xsc", [P, NT, SC])
        xmax, xneg, xsum, xrec = (sb(n, [P, NT]) for n in ("xmax", "xneg", "xsum", "xrec"))
        xp = sb("xp", [P, NT, SC])
        xpT = sb("xpT", [SC, S])
        x2n = sb("x2n", [P, FT, D])
        x2T = (sb("x2T_h", [P, NC, FN], F32R), sb("x2T_l", [P, NC, FN], F32R))
        low = sb("low", [P, FN], F32R)
        gel = [sb(f"gel{i}", [P, FN]) for i in range(4)]
        rank2 = sb("rank2", [P, FN])

        bank = [ctx.enter_context(nc.psum_tensor(f"bank{i}", [P, 512], F32)) for i in range(8)]

        def chunks(t):
            return bank[t][:, :].rearrange("p (c n) -> p c n", c=2)

        w_in, x_in, c_in = sem("weights_loaded"), [sem("x_head_loaded"), sem("x_rest_loaded")], [sem(f"ctx_loaded{i}") for i in range(2)]
        ident_ok, const_ok, w_high, w_low = sem("ident_ok"), sem("const_ok"), sem("w_high"), sem("w_low")
        ln_stats, ln_mv, ln_var, ln_rstd, ln_done = ([sem(f"{n}{i}") for i in range(3)] for n in ("ln_stats", "ln_mv", "ln_var", "ln_rstd", "ln_done"))
        xT_ps, xT_h, xT_l = sem("xT_in_psum"), sem("xT_high"), sem("xT_low")
        qkv_ps = {n: sem(n + "_in_psum") for n in "qkv"}
        full = {n: sem(n + "_full") for n in "qk"}
        part_h, part_m, part_l = ({n: sem(f"{n}_part_{p}") for n in "qk"} for p in "hml")
        rest1 = {n: sem(n + "_rest") for n in "qk"}
        v_ok = sem("v_ready")
        stacked = [sem(f"stacked{i}") for i in range(2)]
        mstacked = [sem(f"max_stacked{i}") for i in range(2)]
        max_ps, max_read = sem("max_scores_in_psum"), sem("max_scores_read")
        msplit, mparts, mT_ps, mT_ok = sem("max_split_step"), sem("max_parts"), sem("maxT_in_psum"), sem("maxT_ready")
        sc_ps, exp_done, av_done, av_evac = sem("scores_in_psum"), sem("probs_ready"), sem("av_group_done"), sem("av_copied")
        att_ps, att_rc, att_ok = sem("att_in_psum"), sem("att_reciprocal"), sem("att_normed")
        attT_ps, attT_h, attT_l = sem("attT_in_psum"), sem("attT_high"), sem("attT_low")
        bo_added, proj_ps, x1_ok = sem("bo_added"), sem("proj_in_psum"), sem("x1_ready")
        x1T_ps, x1T_h, x1T_l = sem("x1T_in_psum"), sem("x1T_high"), sem("x1T_low")
        cT_ps, cT_ok, uq_ps, uq_ok, up_ps, up_ok = (sem(n) for n in ("cT_in_psum", "cT_ready", "uq_in_psum", "uq_ready", "up_in_psum", "up_ready"))
        mask_ok = sem("mask_ok")
        xs_ps, xs_max, xs_neg, xs_exp, xs_rec = (sem(n) for n in ("xs_in_psum", "xs_masked", "xs_negmax", "xs_exp", "xs_reciprocal"))
        xpT_ps, xpT_ok, pv_ps, x2_ok = (sem(n) for n in ("xpT_in_psum", "xpT_ready", "pv_in_psum", "x2_ready"))
        x2T_ps, x2T_h, x2T_l = sem("x2T_in_psum"), sem("x2T_high"), sem("x2T_low")
        low_ps, low_h, low_ok = sem("low_in_psum"), sem("low_high"), sem("low_ready")
        hid_ps, gel_ok, gel_used, r2_ok = (sem(n) for n in ("hidden_in_psum", "gelu_ready", "gelu_used", "rank2_ready"))
        out_ps, b2_added, y_ok, stored = sem("ffn_in_psum"), sem("b2_added"), sem("y_ready"), sem("stored")

        def wait(eng, s, n):
            if not (isinstance(n, int) and n <= 0):
                eng.wait_ge(s, n)

        PAIRS = B // 2
        block = ctx.enter_context(nc.Block())

        def steps(eng, step):
            step(None, None, batch_at(0, 0))
            step(None, batch_at(0, 0), batch_at(0, 1))
            with eng.Fori(0, PAIRS - 1) as pair:
                for k in range(2):
                    step(batch_at(pair, k), batch_at(pair, k + 1), batch_at(pair, k + 2))
            step(batch_at(PAIRS - 1, 0), batch_at(PAIRS - 1, 1), None)
            step(batch_at(PAIRS - 1, 1), None, None)

        @block.sync
        def _(sp):
            sp.dma_start(xres[:, 0:2], io["x"][0:2].rearrange("b (t p) d -> p b t d", p=P)).then_inc(x_in[0], 16)
            for n in ("wq", "wk", "wv"):
                sp.dma_start(weights[n][0][:], io[n].rearrange("(c p) n -> p c n", p=P)).then_inc(w_in, 16)
            sp.dma_start(bq[:], io["bq"]).then_inc(w_in, 16)
            sp.dma_start(bk[:], io["bk"]).then_inc(w_in, 16)
            sp.dma_start(bv[:], io["bv"].partition_broadcast(P)).then_inc(w_in, 16)
            for n in ("wo", "uw"):
                sp.dma_start(weights[n][0][:], io[n].rearrange("(c p) n -> p c n", p=P)).then_inc(w_in, 16)
            sp.dma_start(bo[:], io["bo"].partition_broadcast(P)).then_inc(w_in, 16)
            sp.dma_start(dpar[:], io["dpar"]).then_inc(w_in, 16)
            sp.dma_start(mask_u8[:], io["mask"].partition_broadcast(P)).then_inc(w_in, 16)
            for i in range(2):
                sp.dma_start(cbuf[i][:], io["ctx"][i]).then_inc(c_in[i], 16)
            sp.dma_start(xres[:, 2:B], io["x"][2:B].rearrange("b (t p) d -> p b t d", p=P)).then_inc(x_in[1], 16)
            for half in range(2):
                sp.dma_start(weights["u1"][0][:, :, half * R:(half + 1) * R], io["u1"].rearrange("(c p) n -> p c n", p=P)).then_inc(w_in, 16)
                sp.dma_start(weights["v1"][0][half * R:(half + 1) * R, :], io["v1"]).then_inc(w_in, 16)
                sp.dma_start(v2[half * R:(half + 1) * R, :], io["v2"]).then_inc(w_in, 16)
            sp.dma_start(u2[:], io["u2"].rearrange("(f p) n -> p f n", p=P)).then_inc(w_in, 16)
            sp.dma_start(b1[:], io["b1"]).then_inc(w_in, 16)
            sp.dma_start(b2[:], io["b2"].partition_broadcast(P)).then_inc(w_in, 16)

            def step(late, mid, early):
                if early:
                    e = early
                    for n, parts, which, dst in (("q", qp, Q_PARTS, qs), ("k", kp, K_PARTS, ks)):
                        for level, done in enumerate((part_h, part_m, part_l)):
                            sp.wait_ge(done[n], e.b + 1)
                            for row in (i for i, w in enumerate(which) if w == level):
                                sp.dma_start(
                                    dst[e.parity][row * DH:(row + 1) * DH].rearrange("r (h c) s -> r h (c s)", c=NC),
                                    parts[:, level].rearrange("p c s -> p (c s)")).then_inc(stacked[e.parity], 16)
                if mid:
                    sp.wait_ge(mT_ok, mid.b + 1)
                    sp.dma_start(qs[mid.parity][KR:KM], smax_T[:]).then_inc(mstacked[mid.parity], 16)
                if late and early:
                    sp.wait_ge(pv_ps, late.b + 1)
                    sp.dma_start(cbuf[early.parity][:], io["ctx"][early.b]).then_inc(c_in[early.parity], 16)

            steps(sp, step)

            def store(i):
                sp.wait_ge(y_ok, 2 * i + 2)
                sp.dma_start(io["out"][bass.ds(2 * i, 2)].rearrange("b (t p) d -> p b t d", p=P),
                             xres[:, bass.ds(2 * i, 2)]).then_inc(stored, 16)

            with sp.Fori(0, PAIRS) as i:
                store(i)
            sp.wait_ge(stored, 16 * PAIRS)

        @block.gpsimd
        def _(pool):
            pool.memset(ident[:], 0.0).then_inc(ident_ok, 1)
            pool.memset(ident_bf[:], 0.0).then_inc(ident_ok, 1)
            pool.memset(minus_half[:], -0.5).then_inc(const_ok, 1)
            pool.memset(eps_sb[:], EPS).then_inc(const_ok, 1)
            pool.wait_ge(ident_ok, 2)
            for m in (ident, ident_bf):
                pool.affine_select(out=m[:], in_=m[:], compare_op=ALU.not_equal, fill=1.0, base=0,
                                   pattern=[[-1, P]], channel_multiplier=1).then_inc(ident_ok, 1)
            pool.wait_ge(const_ok, 2)

            def rstd_of(ln, n, tiles):
                pool.wait_ge(ln_mv[ln], n + 1)
                pool.tensor_tensor(var_eps[ln][:, 0:tiles], mv[ln][:, 0:tiles, 1], eps_sb[:, 0:tiles], ALU.add).then_inc(ln_var[ln], 1)
                pool.wait_ge(ln_var[ln], n + 1)
                pool.tensor_tensor(rstd[ln][:, 0:tiles], var_eps[ln][:, 0:tiles], minus_half[:, 0:tiles], ALU.pow).then_inc(ln_rstd[ln], 1)

            def cut(n, whole, rest, parts, e, low_part):
                if not low_part:
                    pool.wait_ge(full[n], e.b + 1)
                    pool.wait_ge(part_h[n], e.b + 1)
                    pool.tensor_tensor(rest[:], whole[:], parts[:, 0], ALU.subtract).then_inc(rest1[n], 1)
                else:
                    pool.wait_ge(part_m[n], e.b + 1)
                    pool.tensor_tensor(parts[:, 2], rest[:], parts[:, 1], ALU.subtract).then_inc(part_l[n], 1)

            def step(late, mid, early):
                if early:
                    rstd_of(0, early.b, NT)
                if late:
                    pool.wait_ge(ln_done[0], late.b + 1)
                    if isinstance(late.b, int) or late.parity == 0:
                        pool.wait_ge(w_in, 16 * W_LOADS)
                    pool.tensor_tensor(xres[:, late.b], xres[:, late.b], bo[:, None, :].to_broadcast([P, NT, D]), ALU.add).then_inc(bo_added, 1)
                if early:
                    cut("q", qf, qr, qp, early, False)
                    cut("q", qf, qr, qp, early, True)
                    cut("k", kf, kr, kp, early, False)
                    cut("k", kf, kr, kp, early, True)
                if late:
                    rstd_of(1, late.b, NT)

            steps(pool, step)

            def ffn(i):
                rstd_of(2, i, FT)
                pool.wait_ge(ln_done[2], i + 1)
                pair = xres[:, bass.ds(2 * i, 2)].rearrange("p b t d -> p (b t) d")
                pool.tensor_tensor(pair, pair, b2[:, None, :].to_broadcast([P, FT, D]), ALU.add).then_inc(b2_added, 1)

            with pool.Fori(0, PAIRS) as i:
                ffn(i)

        @block.vector
        def _(dve):
            for i in range(2):
                dve.memset(vsb[i][:], 0.0).then_inc(const_ok, 1)
                dve.memset(ks[i][:], 1.0).then_inc(const_ok, 1)
            dve.wait_ge(const_ok, 6)
            for i in range(2):
                dve.memset(vsb[i][:, :, :, DH:DH + 1], 1.0).then_inc(const_ok, 1)
            dve.memset(smax_p[:], 0.0).then_inc(const_ok, 1)
            dve.wait_ge(w_in, 16 * W_LOADS)
            for n, (n_w, (whole, high, lo)) in enumerate(weights.items()):
                dve.wait_ge(w_high, n + 1)
                dve.tensor_tensor(lo[:], whole[:], high[:].bitcast(F32), ALU.subtract).then_inc(w_low, 1)

            def layer_norm(ln, n, x, y, tiles, used):
                for t in range(tiles):
                    last = dve.bn_stats(stats[ln][:, t], x[:, t])
                last.then_inc(ln_stats[ln], 1)
                dve.wait_ge(ln_stats[ln], n + 1)
                dve.memset(wait_pad[:], 0.0)
                for t in range(tiles):
                    last = dve.bn_aggr(mv[ln][:, t], stats[ln][:, t])
                last.then_inc(ln_mv[ln], 1)
                used()
                dve.wait_ge(ln_rstd[ln], n + 1)
                for t in range(tiles):
                    last = dve.tensor_scalar(y[:, t], x[:, t], mv[ln][:, t, 0:1], rstd[ln][:, t:t + 1], ALU.subtract, ALU.mult)
                last.then_inc(ln_done[ln], 1)

            def low_part(ps, parts, high_ok, lo_ok, n):
                dve.wait_ge(high_ok, n + 1)
                dve.tensor_tensor(parts[1][:], ps, parts[0][:].bitcast(F32), ALU.subtract).then_inc(lo_ok, 1)

            def step(late, mid, early):
                if early:
                    e = early
                    if isinstance(e.b, int) and e.b == 0:
                        dve.wait_ge(x_in[0], 16)
                    elif not isinstance(e.b, int) and e.parity == 0:
                        dve.wait_ge(x_in[1], 16)
                    layer_norm(0, e.b, xres[:, e.b], xn, NT, lambda: wait(dve, xT_ps, e.b))
                if mid:
                    for h in range(H):
                        dve.wait_ge(max_ps, H * mid.b + h + 1)
                        dve.tensor_reduce(smax[:, :, h], chunks(h % 2), AX.X, ALU.max).then_inc(max_read, 1)
                    dve.wait_ge(max_read, H * (mid.b + 1))
                    dve.tensor_scalar(smax_p[:, :, 0], smax[:], -1.0, None, ALU.mult).then_inc(msplit, 1)
                    dve.wait_ge(msplit, 3 * mid.b + 1)
                    dve.scalar_tensor_tensor(out=smax_r[:], in0=smax[:], scalar=-1.0, in1=smax_p[:, :, 0], op0=ALU.mult, op1=ALU.subtract).then_inc(msplit, 1)
                    dve.wait_ge(msplit, 3 * mid.b + 2)
                    dve.tensor_copy(smax_p[:, :, 1], smax_r[:]).then_inc(msplit, 1)
                    dve.wait_ge(msplit, 3 * mid.b + 3)
                    dve.tensor_tensor(smax_p[:, :, 2], smax_r[:], smax_p[:, :, 1], ALU.subtract).then_inc(mparts, 1)
                if early:
                    low_part(chunks(6), xT, xT_h, xT_l, early.b)
                if late:
                    n = late.b
                    for t in range(NT):
                        rows = bank[2 + t][:, :].rearrange("p (h w) -> p h w", w=W)
                        dve.wait_ge(att_ps, NT * n + t + 1)
                        dve.reciprocal(att_rec[:, t], rows[:, :, DH]).then_inc(att_rc, 1)
                    for t in range(NT):
                        rows = bank[2 + t][:, :].rearrange("p (h w) -> p h w", w=W)
                        dve.wait_ge(att_rc, NT * n + t + 1)
                        dve.tensor_tensor(att[:, t].rearrange("p (h w) -> p h w", w=DH), rows[:, :, 0:DH],
                                          att_rec[:, t, :, None].to_broadcast([P, H, DH]), ALU.mult).then_inc(att_ok, 1)
                    low_part(chunks(5), attT, attT_h, attT_l, n)
                if early:
                    dve.wait_ge(qkv_ps["v"], early.b + 1)
                    dve.tensor_tensor(vsb[early.parity][:, :, :, 0:DH], bank[7][:, :].rearrange("p (t h w) -> p t h w", t=NT, w=DH),
                                      bv[:, None, :].to_broadcast([P, NT, D]).rearrange("p t (h w) -> p t h w", w=DH), ALU.add).then_inc(v_ok, 1)
                if late:
                    dve.wait_ge(proj_ps, n + 1)
                    dve.wait_ge(bo_added, n + 1)
                    dve.tensor_tensor(x1[:], xres[:, n], chunks(4), ALU.add).then_inc(x1_ok, 1)
                    dve.wait_ge(x1_ok, n + 1)
                    layer_norm(1, n, x1, x1n, NT, lambda: None)
                    dve.wait_ge(cT_ps, n + 1)
                    dve.tensor_copy(cT[:], bank[3][:, 0:NC * SC].rearrange("p (c n) -> p c n", c=NC)).then_inc(cT_ok, 1)
                    low_part(chunks(5), x1T, x1T_h, x1T_l, n)
                    dve.wait_ge(uq_ps, n + 1)
                    for c in range(NC):
                        last = dve.tensor_scalar(uqT[:, c], bank[3][:, 256 + c * SC:256 + (c + 1) * SC], 0.0, dpar[:, c:c + 1], ALU.max, ALU.mult)
                    last.then_inc(uq_ok, 1)
                    dve.wait_ge(xs_ps, n + 1)
                    dve.tensor_scalar(neg_mask[:], mask_u8[:, n], MASKED, None, ALU.mult).then_inc(mask_ok, 1)
                    dve.wait_ge(mask_ok, n + 1)
                    dve.memset(wait_pad[:], 0.0)
                    for t in range(NT):
                        last = dve.tensor_tensor_reduce(xsc[:, t], bank[7][:, t * SC:(t + 1) * SC], neg_mask[:], 1.0, MASKED,
                                                        ALU.add, ALU.max, xmax[:, t:t + 1])
                    last.then_inc(xs_max, 1)
                    dve.wait_ge(xs_max, n + 1)
                    dve.tensor_scalar(xneg[:], xmax[:], 4.0, -0.25, ALU.mult, ALU.mult).then_inc(xs_neg, 1)
                    dve.wait_ge(xs_exp, n + 1)
                    dve.reciprocal(xrec[:], xsum[:]).then_inc(xs_rec, 1)
                    dve.wait_ge(xs_rec, n + 1)
                    dve.wait_ge(pv_ps, n + 1)
                    for t in range(NT):
                        last = dve.scalar_tensor_tensor(out=xres[:, n, t], in0=bank[4][:, t * D:(t + 1) * D], scalar=xrec[:, t:t + 1],
                                                        in1=x1[:, t], op0=ALU.mult, op1=ALU.add)
                    last.then_inc(x2_ok, 1)

            steps(dve, step)

            def ffn_in(i, first):
                pair = xres[:, bass.ds(2 * i, 2)].rearrange("p b t d -> p (b t) d")
                if first:
                    dve.wait_ge(x2_ok, B)
                layer_norm(2, i, pair, x2n, FT, lambda: None if first else dve.wait_ge(x2T_ps, NC * i))
                for c in range(NC):
                    dve.wait_ge(x2T_h, NC * i + c + 1)
                    dve.tensor_tensor(x2T[1][:, c], bank[6 + c][:, :], x2T[0][:, c].bitcast(F32), ALU.subtract).then_inc(x2T_l, 1)

            def ffn(i, more):
                dve.wait_ge(low_h, i + 1)
                dve.tensor_tensor(low[R:P], bank[5][R:P, :], low[R:P].bitcast(F32), ALU.subtract).then_inc(low_ok, 1)
                if more:
                    ffn_in(i + 1, False)
                dve.wait_ge(gel_used, NF // 2 * (i + 1))
                dve.tensor_copy(rank2[:], bank[3][:, :]).then_inc(r2_ok, 1)
                for half in range(2):
                    dve.wait_ge(out_ps, 2 * i + half + 1)
                    dve.wait_ge(b2_added, i + 1)
                    y = xres[:, 2 * i + half]
                    dve.tensor_tensor(y, y, chunks((4, 2)[half]), ALU.add).then_inc(y_ok, 1)

            ffn_in(0, True)
            with dve.Fori(0, PAIRS - 1) as i:
                ffn(i, True)
            ffn(PAIRS - 1, False)

        @block.scalar
        def _(act):
            act.wait_ge(w_in, 16 * W_LOADS)
            for whole, high, lo in weights.values():
                act.activation(high[:], whole[:], ACT.Copy).then_inc(w_high, 1)

            def high_part(ps, parts, ps_ok, high_ok, n):
                act.wait_ge(ps_ok, n + 1)
                act.activation(parts[0][:], ps, ACT.Copy).then_inc(high_ok, 1)

            def project_out(n, t, whole, parts, bias, e):
                act.wait_ge(qkv_ps[n], e.b + 1)
                for c in range(NC):
                    last = act.activation(whole[:, c], chunks(t)[:, c], ACT.Identity, bias=bias[:, c:c + 1])
                last.then_inc(full[n], 1)
                for c in range(NC):
                    last = act.activation(parts[:, 0, c], chunks(t)[:, c], ACT.Identity, bias=bias[:, c:c + 1])
                last.then_inc(part_h[n], 1)

            def middle_part(n, rest, parts, e):
                act.wait_ge(rest1[n], e.b + 1)
                act.activation(parts[:, 1], rest[:], ACT.Copy).then_inc(part_m[n], 1)

            def step(late, mid, early):
                if late:
                    n = late.b
                    for h in range(H):
                        g = h // HG
                        if h % HG == 0 and g >= 2:
                            act.wait_ge(av_done, NG * n + g - 1)
                        act.wait_ge(sc_ps, H * n + h + 1)
                        act.activation(probs[g % 2][:, h % HG], chunks(2 + h % 2), ACT.Exp, scale=SCALE).then_inc(exp_done, 1)
                        if h == 11:
                            act.wait_ge(av_done, NG * n + 2)
                            act.activation(att_raw[:, 0:2], chunks(4), ACT.Copy).then_inc(av_evac, 1)
                    act.wait_ge(av_done, NG * n + 4)
                    act.activation(att_raw[:, 2:4], chunks(5), ACT.Copy).then_inc(av_evac, 1)
                if early:
                    high_part(chunks(6), xT, xT_ps, xT_h, early.b)
                    project_out("q", 0, qf, qp, bq, early)
                if late:
                    high_part(chunks(5), attT, attT_ps, attT_h, n)
                if early:
                    middle_part("q", qr, qp, early)
                    project_out("k", 1, kf, kp, bk, early)
                if mid:
                    act.wait_ge(mT_ps, mid.b + 1)
                    act.activation(smax_T[:], bank[6][0:3 * H, 0:S // 2].bitcast(BF16), ACT.Copy).then_inc(mT_ok, 1)
                if early:
                    middle_part("k", kr, kp, early)
                if late:
                    high_part(chunks(5), x1T, x1T_ps, x1T_h, n)
                    act.wait_ge(up_ps, n + 1)
                    act.activation(upT[:], chunks(2), ACT.Relu).then_inc(up_ok, 1)
                    act.wait_ge(xs_neg, n + 1)
                    for t in range(NT):
                        last = act.activation(xp[:, t], xsc[:, t], ACT.Exp, bias=xneg[:, t:t + 1], accum_out=xsum[:, t:t + 1])
                    last.then_inc(xs_exp, 1)
                    act.wait_ge(xpT_ps, n + 1)
                    act.activation(xpT[:], bank[6][0:SC, 0:S], ACT.Copy).then_inc(xpT_ok, 1)

            steps(act, step)

            def ffn_in(i):
                for c in range(NC):
                    act.wait_ge(x2T_ps, NC * i + c + 1)
                    act.activation(x2T[0][:, c], bank[6 + c][:, :], ACT.Copy).then_inc(x2T_h, 1)

            def ffn(i, more):
                act.wait_ge(low_ps, i + 1)
                act.activation(low[:], bank[5][:, :], ACT.Copy).then_inc(low_h, 1)
                for f in range(NF):
                    act.wait_ge(hid_ps, NF * i + f + 1)
                    if f >= 4:
                        act.wait_ge(gel_used, NF // 2 * i + (f - 4) // 2 + 1)
                    act.activation(gel[f % 4][:], bank[f % 2][:, :], ACT.Gelu_apprx_tanh, bias=b1[:, f:f + 1]).then_inc(gel_ok, 1)
                    if f == NF - 3 and more:
                        ffn_in(i + 1)

            ffn_in(0)
            with act.Fori(0, PAIRS - 1) as i:
                ffn(i, True)
            ffn(PAIRS - 1, False)

        @block.tensor
        def _(pe):
            pe.wait_ge(ident_ok, 4)
            pe.wait_ge(const_ok, 9)
            pe.wait_ge(w_low, len(weights))
            parts_of = {n: (h, l) for n, (_, h, l) in weights.items()}

            def products(out, left, right, first=True, last=True):
                terms = ((0, 0), (0, 1), (1, 0))
                for n, (i, j) in enumerate(terms):
                    mm = pe.matmul(out, left[i], right[j], start=first and n == 0, stop=last and n == len(terms) - 1)
                return mm

            def to_channels(t, x, tiles):
                for c in range(NC):
                    for k in range(tiles):
                        last = pe.transpose(bank[t][:, c * S + k * P:c * S + (k + 1) * P], x[:, k, c * P:(c + 1) * P], ident[:])
                return last

            def project_rows(t, name, x):
                w = parts_of[name]
                for m in range(NC):
                    for c in range(NC):
                        last = products(chunks(t)[:, m], [w[i][:, c, m * P:(m + 1) * P] for i in range(2)], [x[i][:, c] for i in range(2)], c == 0, c == NC - 1)
                return last

            def project_tokens(t, name, x):
                w = parts_of[name]
                for k in range(NT):
                    for c in range(NC):
                        last = products(chunks(t)[:, k], [x[i][:, c, k * P:(k + 1) * P] for i in range(2)], [w[i][:, c] for i in range(2)], c == 0, c == NC - 1)
                return last

            def max_scores(m, h):
                if h < 2:
                    if h == 0:
                        pe.wait_ge(stacked[m.parity], 2 * NP * 16 * (m.turn + 1))
                        pe.wait_ge(part_h["q"], m.b + 1)
                        pe.wait_ge(part_h["k"], m.b + 1)
                else:
                    pe.wait_ge(max_read, H * m.b + h - 1)
                for t in range(NT):
                    last = pe.matmul(chunks(h % 2)[:, t], qs[m.parity][0:KR, h, t * P:(t + 1) * P], ks[m.parity][0:KR, h], start=True, stop=True)
                last.then_inc(max_ps, 1)

            def scores(s, h):
                if h == 0:
                    pe.wait_ge(mstacked[s.parity], 16 * (s.turn + 1))
                if h >= 2:
                    pe.wait_ge(exp_done, H * s.b + h - 1)
                for t in range(NT):
                    last = pe.matmul(chunks(2 + h % 2)[:, t], ks[s.parity][0:KM, h, t * P:(t + 1) * P], qs[s.parity][0:KM, h], start=True, stop=True)
                last.then_inc(sc_ps, 1)

            def attend(s, g):
                pe.wait_ge(exp_done, H * s.b + HG * (g + 1))
                for t in range(NT):
                    for j in range(HG):
                        last = pe.matmul(chunks(4 + g // 2)[j * W:(j + 1) * W, g % 2], vsb[s.parity][:, t, HG * g + j], probs[g % 2][:, j, t],
                                         start=t == 0, stop=t == NT - 1, tile_position=(0, j * W))
                last.then_inc(av_done, 1)

            def step(late, mid, early):
                for h in range(H):
                    if mid:
                        max_scores(mid, h)
                    if late:
                        scores(late, h)
                        if h % HG == 1 and h > HG:
                            if h == HG + 1 and not mid:
                                pe.wait_ge(x2_ok, late.b)
                            attend(late, h // HG - 1)
                if late:
                    n = late.b
                    attend(late, NG - 1)
                if early:
                    pe.wait_ge(ln_done[0], early.b + 1)
                    to_channels(6, xn, NT).then_inc(xT_ps, 1)
                if late:
                    pe.wait_ge(av_evac, 2 * n + 2)
                    for t in range(NT):
                        for g in range(NG):
                            last = pe.transpose(bank[2 + t][:, g * P:(g + 1) * P], att_raw[:, g, t * P:(t + 1) * P], ident[:])
                        last.then_inc(att_ps, 1)
                if early:
                    if mid:
                        pe.wait_ge(max_read, H * (mid.b + 1))
                    pe.wait_ge(xT_l, early.b + 1)
                    project_rows(0, "wq", xT).then_inc(qkv_ps["q"], 1)
                if late:
                    pe.wait_ge(att_ok, NT * (n + 1))
                    to_channels(5, att, NT).then_inc(attT_ps, 1)
                if early:
                    project_rows(1, "wk", xT).then_inc(qkv_ps["k"], 1)
                if mid:
                    pe.wait_ge(mparts, mid.b + 1)
                    for t in range(NT):
                        last = pe.transpose(bank[6][0:5 * H, t * P // 2:(t + 1) * P // 2].bitcast(BF16),
                                            smax_p[:, t].rearrange("p k h -> p (k h)"), ident_bf[:])
                    last.then_inc(mT_ps, 1)
                if late:
                    pe.wait_ge(attT_l, n + 1)
                    project_tokens(4, "wo", attT).then_inc(proj_ps, 1)
                if early:
                    project_tokens(7, "wv", xT).then_inc(qkv_ps["v"], 1)
                if late:
                    pe.wait_ge(c_in[late.parity], 16 * (late.turn + 1))
                    for c in range(NC):
                        last = pe.transpose(bank[3][:, c * SC:(c + 1) * SC], cbuf[late.parity][:, c * P:(c + 1) * P], ident[0:SC, 0:SC])
                    last.then_inc(cT_ps, 1)
                    pe.wait_ge(ln_done[1], n + 1)
                    to_channels(5, x1n, NT).then_inc(x1T_ps, 1)
                    pe.wait_ge(cT_ok, n + 1)
                    for m in range(NC):
                        for c in range(NC):
                            last = pe.matmul(bank[3][:, 256 + m * SC:256 + (m + 1) * SC], weights["uw"][0][:, c, m * P:(m + 1) * P], cT[:, c],
                                             start=c == 0, stop=c == NC - 1)
                    last.then_inc(uq_ps, 1)
                    pe.wait_ge(x1T_l, n + 1)
                    project_rows(2, "uw", x1T).then_inc(up_ps, 1)
                    pe.wait_ge(uq_ok, n + 1)
                    pe.wait_ge(up_ok, n + 1)
                    if early:
                        pe.wait_ge(v_ok, early.b + 1)
                    for t in range(NT):
                        for c in range(NC):
                            last = pe.matmul(bank[7][:, t * SC:(t + 1) * SC], upT[:, c, t * P:(t + 1) * P], uqT[:, c], start=c == 0, stop=c == NC - 1)
                    last.then_inc(xs_ps, 1)
                    pe.wait_ge(xs_exp, n + 1)
                    if mid:
                        pe.wait_ge(mT_ok, mid.b + 1)
                    for t in range(NT):
                        last = pe.transpose(bank[6][0:SC, t * P:(t + 1) * P], xp[:, t], ident[:])
                    last.then_inc(xpT_ps, 1)
                    pe.wait_ge(xpT_ok, n + 1)
                    for t in range(NT):
                        last = pe.matmul(chunks(4)[:, t], xpT[:, t * P:(t + 1) * P], cbuf[late.parity][:], start=True, stop=True)
                    last.then_inc(pv_ps, 1)

            steps(pe, step)

            def ffn_in(i):
                pe.wait_ge(ln_done[2], i + 1)
                for c in range(NC):
                    for t in range(FT):
                        last = pe.transpose(bank[6 + c][:, t * P:(t + 1) * P], x2n[:, t, c * P:(c + 1) * P], ident[:])
                    last.then_inc(x2T_ps, 1)

            def ffn(i, more):
                pe.wait_ge(x2T_l, NC * (i + 1))
                u1 = parts_of["u1"]
                for c in range(NC):
                    last = products(bank[5][:, :], [u1[k][:, c] for k in range(2)], [x2T[k][:, c] for k in range(2)], c == 0, c == NC - 1)
                last.then_inc(low_ps, 1)
                pe.wait_ge(low_ok, i + 1)

                def hidden(f):
                    if f >= 2:
                        pe.wait_ge(gel_ok, NF * i + f - 1)
                    for k in range(2):
                        last = pe.matmul(bank[f % 2][:, :], parts_of["v1"][k][:, f * P:(f + 1) * P], low[:], start=k == 0, stop=k == 1)
                    last.then_inc(hid_ps, 1)

                def rank(f):
                    pe.wait_ge(gel_ok, NF * i + f + 2)
                    for k in range(2):
                        last = pe.matmul(bank[3][k * R:(k + 1) * R, :], u2[:, f + k], gel[(f + k) % 4][:], start=f == 0, stop=f == NF - 2,
                                         tile_position=(0, k * R))
                    last.then_inc(gel_used, 1)
                    return last

                hidden(0)
                hidden(1)
                for f in range(0, NF, 2):
                    if f + 2 < NF:
                        hidden(f + 2)
                        hidden(f + 3)
                    elif more:
                        ffn_in(i + 1)
                    rank(f)
                pe.wait_ge(r2_ok, i + 1)
                for half in range(2):
                    for t in range(NT):
                        k = half * NT + t
                        last = pe.matmul(chunks((4, 2)[half])[:, t], rank2[:, k * P:(k + 1) * P], v2[:], start=True, stop=True)
                    last.then_inc(out_ps, 1)

            ffn_in(0)
            with pe.Fori(0, PAIRS - 1) as i:
                ffn(i, True)
            ffn(PAIRS - 1, False)


INS = ("x", "ctx", "mask", "wq", "wk", "wv", "wo", "uw", "bq", "bk", "bv", "bo", "dpar", "u1", "v1", "b1", "u2", "v2", "b2")


def kernel(x, ctx_1024, mask_BxS2_bf0, mask_BxS2_bk1, L0_attn_Wq, L0_attn_bq, L0_attn_Wk, L0_attn_bk, L0_attn_Wv, L0_attn_bv,
           L0_attn_Wo, L0_attn_bo, L0_xattn_U_w, L0_xattn_D_param, L0_ffn_U1, L0_ffn_V1, L0_ffn_b1, L0_ffn_U2, L0_ffn_V2, L0_ffn_b2):
    import concourse.bacc as bacc
    from concourse.bass_utils import run_bass_kernel_spmd

    heads, D = 16, x.shape[-1]
    chunks, dh = D // P, D // heads

    def head_minor(w):
        w = np.asarray(w)
        return np.moveaxis(w.reshape(heads // chunks, chunks, dh, *w.shape[1:]), 0, 2).reshape(w.shape)

    def columns(v):
        return np.asarray(v).reshape(-1, P).T

    laid = {
        "x": x, "ctx": ctx_1024, "mask": mask_BxS2_bk1,
        "wq": head_minor(L0_attn_Wq).T, "wk": head_minor(L0_attn_Wk).T, "wv": np.asarray(L0_attn_Wv).T, "wo": np.asarray(L0_attn_Wo).T,
        "uw": np.asarray(L0_xattn_U_w).T, "bq": columns(head_minor(L0_attn_bq)), "bk": columns(head_minor(L0_attn_bk)),
        "bv": L0_attn_bv, "bo": L0_attn_bo, "dpar": columns(L0_xattn_D_param), "u1": L0_ffn_U1, "v1": L0_ffn_V1,
        "b1": columns(L0_ffn_b1), "u2": L0_ffn_U2, "v2": L0_ffn_V2, "b2": L0_ffn_b2,
    }
    nc = bacc.Bacc("TRN2", target_bir_lowering=False, num_devices=1)
    arrays, io = {}, {}
    for name in INS:
        a = np.ascontiguousarray(laid[name])
        arrays[f"in_{name}"] = a
        io[name] = nc.dram_tensor(f"in_{name}", a.shape, mybir.dt.from_np(a.dtype), kind="ExternalInput").ap()
    io["out"] = nc.dram_tensor("out_y", x.shape, F32, kind="ExternalOutput").ap()
    decoder_layer(nc, io)
    return run_bass_kernel_spmd(nc, [arrays], core_ids=[0]).results[0]["out_y"]
```

```python
from contextlib import ExitStack

import numpy as np
import concourse.bass as bass
from concourse import mybir

ALU = mybir.AluOpType
ACT = mybir.ActivationFunctionType
AX = mybir.AxisListType
F32 = mybir.dt.float32
F32R = mybir.dt.float32r
BF16 = mybir.dt.bfloat16
U8 = mybir.dt.uint8

P = 128
EPS = 1e-5
MASKED = -3.0e38
Q_PARTS = (0, 0, 0, 1, 1, 2)
K_PARTS = (0, 1, 2, 0, 1, 0)


class Batch:

    def __init__(self, b, parity, turn):
        self.b, self.parity, self.turn = b, parity, turn


def batch_at(pair, k):
    return Batch(2 * pair + k, k % 2, pair + k // 2)


def decoder_layer(nc, io):
    B, S, D = io["x"].shape
    SC = io["ctx"].shape[1]
    NT, NC = S // P, D // P
    H, DH = 16, D // 16
    HC = H // NC
    HG = 4
    NG = H // HG
    W = 32
    F = io["b1"].shape[0] * io["b1"].shape[1]
    NF = F // P
    R = io["u1"].shape[-1]
    NP = len(Q_PARTS)
    KR = NP * DH
    KM = KR + 3
    SCALE = float(DH) ** -0.5
    FT = 2 * NT
    FN = FT * P
    LOADS = {"u1": 2, "v1": 2, "attention": 3, "ffn": 5}
    assert S == 2 * P and D == 2 * P and R == 64 and H % HG == 0 and B % 2 == 0

    ctx = ExitStack()
    with ctx:
        def sb(name, shape, dt=F32):
            return ctx.enter_context(nc.sbuf_tensor(name, shape, dt))

        def sem(name):
            return ctx.enter_context(nc.semaphore(name))

        ident = sb("ident", [P, P])
        ident_bf = sb("ident_bf", [P, P], BF16)
        weights = {}
        for n, cols in (("wq", D), ("wk", D), ("wv", D), ("uw", D), ("wo", D), ("u1", P)):
            weights[n] = (sb(n + "_f", [P, NC, cols]), sb(n + "_h", [P, NC, cols], F32R), sb(n + "_l", [P, NC, cols], F32R))
        weights["v1"] = (sb("v1_f", [P, F]), sb("v1_h", [P, F], F32R), sb("v1_l", [P, F], F32R))
        u2 = sb("u2", [P, NF, R])
        v2 = sb("v2", [P, D])
        bq, bk, dpar = sb("bq_sb", [P, NC]), sb("bk_sb", [P, NC]), sb("dpar_sb", [P, NC])
        b1 = sb("b1_sb", [P, NF])
        bv, bo, b2 = sb("bv_sb", [P, D]), sb("bo_sb", [P, D]), sb("b2_sb", [P, D])
        mask_u8 = sb("mask_u8", [P, B, SC], U8)
        neg_mask = sb("neg_mask", [P, SC])
        wait_pad = sb("wait_pad", [P, 1])
        minus_half, eps_sb = sb("minus_half", [P, FT]), sb("eps", [P, FT])

        xres = sb("xres", [P, B, NT, D])
        cbuf = [sb(f"cbuf{i}", [SC, D]) for i in range(2)]
        stats = [sb(f"stats{i}", [P, FT, 6]) for i in range(3)]
        mv = [sb(f"mv{i}", [P, FT, 2]) for i in range(3)]
        var_eps = [sb(f"var_eps{i}", [P, FT]) for i in range(3)]
        rstd = [sb(f"rstd{i}", [P, FT]) for i in range(3)]
        xn = sb("xn", [P, NT, D])
        xT = (sb("xT_h", [P, NC, S], F32R), sb("xT_l", [P, NC, S], F32R))
        qf, kf = sb("qf", [P, NC, S]), sb("kf", [P, NC, S])
        qr, kr = sb("qr", [P, NC, S]), sb("kr", [P, NC, S])
        qp = [sb(f"qp{i}", [P, 3, NC, S], BF16) for i in range(2)]
        kp = [sb(f"kp{i}", [P, 3, NC, S], BF16) for i in range(2)]
        qs = [sb(f"qs{i}", [P, H, S], BF16) for i in range(2)]
        ks = [sb(f"ks{i}", [P, H, S], BF16) for i in range(2)]
        vsb = [sb(f"v{i}", [P, NT, H, W]) for i in range(2)]
        smax = sb("smax", [P, NT, H])
        smax_r = sb("smax_r", [P, NT, H])
        smax_p = sb("smax_p", [P, NT, 5, H], BF16)
        smax_T = sb("smax_T", [3 * H, S], BF16)
        probs = [sb(f"probs{i}", [P, HG, NT, S]) for i in range(2)]
        att_raw = sb("att_raw", [P, NG, S])
        att_rec = sb("att_rec", [P, NT, H])
        att = sb("att", [P, NT, D])
        attT = (sb("attT_h", [P, NC, S], F32R), sb("attT_l", [P, NC, S], F32R))
        x1 = sb("x1", [P, NT, D])
        x1n = sb("x1n", [P, NT, D])
        x1T = (sb("x1T_h", [P, NC, S], F32R), sb("x1T_l", [P, NC, S], F32R))
        cT = sb("cT", [P, NC, SC])
        upT = sb("upT", [P, NC, S])
        uqT = sb("uqT", [P, NC, SC])
        xsc = sb("xsc", [P, NT, SC])
        xmax, xneg, xsum, xrec = (sb(n, [P, NT]) for n in ("xmax", "xneg", "xsum", "xrec"))
        xp = sb("xp", [P, NT, SC])
        xpT = sb("xpT", [SC, S])
        x2n = sb("x2n", [P, FT, D])
        x2T = (sb("x2T_h", [P, NC, FN], F32R), sb("x2T_l", [P, NC, FN], F32R))
        low = sb("low", [P, FN], F32R)
        gel = [sb(f"gel{i}", [P, FN]) for i in range(4)]
        rank2 = sb("rank2", [P, FN])

        bank = [ctx.enter_context(nc.psum_tensor(f"bank{i}", [P, 512], F32)) for i in range(8)]

        def chunks(t):
            return bank[t][:, :].rearrange("p (c n) -> p c n", c=2)

        w_in = {n: sem(n + "_loaded") for n in (*weights, "bq", "bk", "bv", "attention", "ffn")}
        x_in, c_in = [sem(f"x_loaded{i}") for i in range(3)], [sem(f"ctx_loaded{i}") for i in range(2)]
        v_zero = sem("buffers_zeroed")
        ident_ok, const_ok, w_high, w_low = sem("ident_ok"), sem("const_ok"), sem("w_high"), sem("w_low")
        ln_stats, ln_mv, ln_var, ln_rstd, ln_done = ([sem(f"{n}{i}") for i in range(3)] for n in ("ln_stats", "ln_mv", "ln_var", "ln_rstd", "ln_done"))
        xT_ps, xT_h, xT_l = sem("xT_in_psum"), sem("xT_high"), sem("xT_low")
        qkv_ps = {n: sem(n + "_in_psum") for n in "qkv"}
        full = {n: sem(n + "_full") for n in "qk"}
        part_h, part_m, part_l = ({n: sem(f"{n}_part_{p}") for n in "qk"} for p in "hml")
        rest1 = {n: sem(n + "_rest") for n in "qk"}
        v_ok = sem("v_ready")
        stacked = [[sem(f"stacked{i}_heads{j}") for j in range(2)] for i in range(2)]
        mstacked = [sem(f"max_stacked{i}") for i in range(2)]
        max_ps, max_read = sem("max_scores_in_psum"), sem("max_scores_read")
        msplit, mparts, mT_ps, mT_ok = sem("max_split_step"), sem("max_parts"), sem("maxT_in_psum"), sem("maxT_ready")
        sc_ps, exp_done, av_done, av_evac = sem("scores_in_psum"), sem("probs_ready"), sem("av_group_done"), sem("av_copied")
        att_ps, att_rc, att_ok = sem("att_in_psum"), sem("att_reciprocal"), sem("att_normed")
        attT_ps, attT_h, attT_l = sem("attT_in_psum"), sem("attT_high"), sem("attT_low")
        bo_added, proj_ps, x1_ok = sem("bo_added"), sem("proj_in_psum"), sem("x1_ready")
        x1T_ps, x1T_h, x1T_l = sem("x1T_in_psum"), sem("x1T_high"), sem("x1T_low")
        cT_ps, cT_ok, uq_ps, uq_ok, up_ps, up_ok = (sem(n) for n in ("cT_in_psum", "cT_ready", "uq_in_psum", "uq_ready", "up_in_psum", "up_ready"))
        mask_ok = sem("mask_ok")
        xs_ps, xs_max, xs_neg, xs_exp, xs_rec = (sem(n) for n in ("xs_in_psum", "xs_masked", "xs_negmax", "xs_exp", "xs_reciprocal"))
        xpT_ps, xpT_ok, pv_ps, x2_ok = (sem(n) for n in ("xpT_in_psum", "xpT_ready", "pv_in_psum", "x2_ready"))
        x2T_ps, x2T_h, x2T_l = sem("x2T_in_psum"), sem("x2T_high"), sem("x2T_low")
        low_ps, low_h, low_ok = sem("low_in_psum"), sem("low_high"), sem("low_ready")
        hid_ps, gel_ok, gel_used, r2_ok = (sem(n) for n in ("hidden_in_psum", "gelu_ready", "gelu_used", "rank2_ready"))
        out_ps, b2_added, y_ok, stored = sem("ffn_in_psum"), sem("b2_added"), sem("y_ready"), sem("stored")

        def wait(eng, s, n):
            if not (isinstance(n, int) and n <= 0):
                eng.wait_ge(s, n)

        PAIRS = B // 2
        block = ctx.enter_context(nc.Block())

        def steps(eng, between, heads, last):
            def at(b):
                return [batch_at(0, b + d) if 0 <= b + d < B else None for d in range(4)]

            for b in range(-3, 0):
                between(*at(b))
                heads(*at(b))
            whole = (B - 3) // 2
            with eng.Fori(0, whole) as pair:
                for k in range(2):
                    now = [batch_at(pair, k + d) for d in range(4)]
                    between(*now)
                    heads(*now)
            for b in range(2 * whole, B - 1):
                between(*at(b))
                heads(*at(b))
            between(*at(B - 1))
            last(at(B - 1)[0])

        @block.sync
        def _(sp):
            sp.dma_start(xres[:, 0:1], io["x"][0:1].rearrange("b (t p) d -> p b t d", p=P)).then_inc(x_in[0], 16)
            for n in ("wq", "wk", "wv"):
                sp.dma_start(weights[n][0][:], io[n].rearrange("(c p) n -> p c n", p=P)).then_inc(w_in[n], 16)
            sp.dma_start(xres[:, 1:2], io["x"][1:2].rearrange("b (t p) d -> p b t d", p=P)).then_inc(x_in[1], 16)
            for n in ("uw", "wo"):
                sp.dma_start(weights[n][0][:], io[n].rearrange("(c p) n -> p c n", p=P)).then_inc(w_in[n], 16)
            sp.dma_start(xres[:, 2:B], io["x"][2:B].rearrange("b (t p) d -> p b t d", p=P)).then_inc(x_in[2], 16)
            for half in range(2):
                sp.dma_start(weights["u1"][0][:, :, half * R:(half + 1) * R], io["u1"].rearrange("(c p) n -> p c n", p=P)).then_inc(w_in["u1"], 16)
                sp.dma_start(weights["v1"][0][half * R:(half + 1) * R, :], io["v1"]).then_inc(w_in["v1"], 16)
                sp.dma_start(v2[half * R:(half + 1) * R, :], io["v2"]).then_inc(w_in["ffn"], 16)
            sp.dma_start(u2[:], io["u2"].rearrange("(f p) n -> p f n", p=P)).then_inc(w_in["ffn"], 16)
            sp.dma_start(b1[:], io["b1"]).then_inc(w_in["ffn"], 16)
            sp.dma_start(b2[:], io["b2"].partition_broadcast(P)).then_inc(w_in["ffn"], 16)

            cuts = (("k", 0, part_h), ("q", 0, part_h), ("q", 1, part_m), ("q", 2, part_l), ("k", 1, part_m), ("k", 2, part_l))
            stacks = {"q": (qp, Q_PARTS, qs), "k": (kp, K_PARTS, ks)}

            def stack(e, half):
                for n, level, done in cuts:
                    parts, which, dst = stacks[n]
                    if half == 0:
                        sp.wait_ge(done[n], e.b + 1)
                    for row in (i for i, w in enumerate(which) if w == level):
                        sp.dma_start(
                            dst[e.parity][row * DH:(row + 1) * DH, half * H // 2:(half + 1) * H // 2].rearrange("r (h c) s -> r h (c s)", c=NC),
                            parts[e.parity][half * P // 2:(half + 1) * P // 2, level].rearrange("p c s -> p (c s)")).then_inc(stacked[e.parity][half], 16)

            def heads(post, late, mid, early):
                if early:
                    stack(early, 0)
                if post and mid:
                    sp.wait_ge(pv_ps, post.b + 1)
                    sp.dma_start(cbuf[mid.parity][:], io["ctx"][mid.b]).then_inc(c_in[mid.parity], 16)

            def between(post, late, mid, early):
                if mid:
                    if post:
                        sp.wait_ge(sc_ps, H * (post.b + 1))
                    stack(mid, 1)

            steps(sp, between, heads, lambda post: None)

            def store(b):
                sp.wait_ge(y_ok, b + 1)
                sp.dma_start(io["out"][bass.ds(b, 1)].rearrange("b (t p) d -> p b t d", p=P), xres[:, bass.ds(b, 1)]).then_inc(stored, 16)

            with sp.Fori(0, B) as b:
                store(b)
            sp.wait_ge(stored, 16 * B)

        @block.gpsimd
        def _(pool):
            pool.memset(ident[:], 0.0).then_inc(ident_ok, 1)
            pool.memset(ident_bf[:], 0.0).then_inc(ident_ok, 1)
            pool.memset(minus_half[:], -0.5).then_inc(const_ok, 1)
            pool.memset(eps_sb[:], EPS).then_inc(const_ok, 1)
            pool.wait_ge(ident_ok, 2)
            for m in (ident, ident_bf):
                pool.affine_select(out=m[:], in_=m[:], compare_op=ALU.not_equal, fill=1.0, base=0,
                                   pattern=[[-1, P]], channel_multiplier=1).then_inc(ident_ok, 1)
            pool.wait_ge(const_ok, 2)
            pool.wait_ge(ident_ok, 4)

            def rstd_of(ln, n, tiles):
                pool.wait_ge(ln_mv[ln], n + 1)
                pool.tensor_tensor(var_eps[ln][:, 0:tiles], mv[ln][:, 0:tiles, 1], eps_sb[:, 0:tiles], ALU.add).then_inc(ln_var[ln], 1)
                pool.wait_ge(ln_var[ln], n + 1)
                pool.tensor_tensor(rstd[ln][:, 0:tiles], var_eps[ln][:, 0:tiles], minus_half[:, 0:tiles], ALU.pow).then_inc(ln_rstd[ln], 1)

            def cut(n, whole, rest, parts, e, low_part):
                if not low_part:
                    pool.wait_ge(full[n], e.b + 1)
                    pool.wait_ge(part_h[n], e.b + 1)
                    pool.tensor_tensor(rest[:], whole[:], parts[e.parity][:, 0], ALU.subtract).then_inc(rest1[n], 1)
                else:
                    pool.wait_ge(part_m[n], e.b + 1)
                    pool.tensor_tensor(parts[e.parity][:, 2], rest[:], parts[e.parity][:, 1], ALU.subtract).then_inc(part_l[n], 1)

            def heads(post, late, mid, early):
                if post:
                    rstd_of(1, post.b, NT)
                if late:
                    if isinstance(late.b, int) and late.b == 0:
                        pool.wait_ge(w_in["attention"], 16 * LOADS["attention"])
                    pool.wait_ge(ln_done[0], late.b + 1)
                    pool.tensor_tensor(xres[:, late.b], xres[:, late.b], bo[:, None, :].to_broadcast([P, NT, D]), ALU.add).then_inc(bo_added, 1)
                if early:
                    cut("q", qf, qr, qp, early, False)
                    cut("q", qf, qr, qp, early, True)
                    cut("k", kf, kr, kp, early, False)
                    cut("k", kf, kr, kp, early, True)

                if late and not mid:
                    for i in range(2):
                        rstd_of(2, i, FT)

            def between(post, late, mid, early):
                if early:
                    rstd_of(0, early.b, NT)

            def ffn(i, post, more):
                if post:
                    rstd_of(1, post.b, NT)
                elif more:
                    rstd_of(2, i + 1, FT)
                pool.wait_ge(ln_done[2], i + 1)
                pair = xres[:, bass.ds(2 * i, 2)].rearrange("p b t d -> p (b t) d")
                pool.tensor_tensor(pair, pair, b2[:, None, :].to_broadcast([P, FT, D]), ALU.add).then_inc(b2_added, 1)

            def ffn_first(post):
                pool.wait_ge(w_in["ffn"], 16 * LOADS["ffn"])
                ffn(0, post, True)

            steps(pool, between, heads, ffn_first)
            with pool.Fori(1, PAIRS - 1) as i:
                ffn(i, None, True)
            ffn(PAIRS - 1, None, False)

        @block.vector
        def _(dve):
            def fill_buffers():
                for i in range(2):
                    dve.memset(vsb[i][:], 0.0).then_inc(v_zero, 1)
                dve.memset(smax_p[:], 0.0).then_inc(v_zero, 1)
                dve.wait_ge(v_zero, 3)
                for i in range(2):
                    dve.memset(vsb[i][:, :, :, DH:DH + 1], 1.0).then_inc(v_zero, 1)

            def weight_low(n, order=tuple(weights)):
                whole, high, lo = weights[n]
                dve.wait_ge(w_high, order.index(n) + 1)
                dve.tensor_tensor(lo[:], whole[:], high[:].bitcast(F32), ALU.subtract).then_inc(w_low, 1)

            def norm_stats(ln, n, x, tiles):
                for t in range(tiles):
                    last = dve.bn_stats(stats[ln][:, t], x[:, t])
                last.then_inc(ln_stats[ln], 1)
                dve.wait_ge(ln_stats[ln], n + 1)
                dve.memset(wait_pad[:], 0.0)
                for t in range(tiles):
                    last = dve.bn_aggr(mv[ln][:, t], stats[ln][:, t])
                last.then_inc(ln_mv[ln], 1)

            def norm_apply(ln, n, x, y, tiles):
                dve.wait_ge(ln_rstd[ln], n + 1)
                for t in range(tiles):
                    last = dve.tensor_scalar(y[:, t], x[:, t], mv[ln][:, t, 0:1], rstd[ln][:, t:t + 1], ALU.subtract, ALU.mult)
                last.then_inc(ln_done[ln], 1)

            def low_part(ps, parts, high_ok, lo_ok, n):
                dve.wait_ge(high_ok, n + 1)
                dve.tensor_tensor(parts[1][:], ps, parts[0][:].bitcast(F32), ALU.subtract).then_inc(lo_ok, 1)

            def maximum(mid, h):
                dve.wait_ge(max_ps, H * mid.b + h + 1)
                dve.tensor_reduce(smax[:, :, h], chunks(h % 2), AX.X, ALU.max).then_inc(max_read, 1)

            def post_uq(p):
                dve.wait_ge(uq_ps, p.b + 1)
                for c in range(NC):
                    last = dve.tensor_scalar(uqT[:, c], bank[7][:, 256 + c * SC:256 + (c + 1) * SC], 0.0, dpar[:, c:c + 1], ALU.max, ALU.mult)
                last.then_inc(uq_ok, 1)

            def post_mask(p, scores):
                dve.wait_ge(xs_ps, p.b + 1)
                dve.tensor_scalar(neg_mask[:], mask_u8[:, p.b], MASKED, None, ALU.mult).then_inc(mask_ok, 1)
                dve.wait_ge(mask_ok, p.b + 1)
                dve.memset(wait_pad[:], 0.0)
                for t in range(NT):
                    last = dve.tensor_tensor_reduce(xsc[:, t], bank[scores][:, t * SC:(t + 1) * SC], neg_mask[:], 1.0, MASKED,
                                                    ALU.add, ALU.max, xmax[:, t:t + 1])
                last.then_inc(xs_max, 1)
                dve.wait_ge(xs_max, p.b + 1)
                dve.tensor_scalar(xneg[:], xmax[:], 4.0, -0.25, ALU.mult, ALU.mult).then_inc(xs_neg, 1)

            def post_sum(p):
                dve.wait_ge(xs_exp, p.b + 1)
                dve.reciprocal(xrec[:], xsum[:]).then_inc(xs_rec, 1)

            def post_add(p, values):
                dve.wait_ge(xs_rec, p.b + 1)
                dve.wait_ge(pv_ps, p.b + 1)
                for t in range(NT):
                    last = dve.scalar_tensor_tensor(out=xres[:, p.b, t], in0=bank[values][:, t * D:(t + 1) * D], scalar=xrec[:, t:t + 1],
                                                    in1=x1[:, t], op0=ALU.mult, op1=ALU.add)
                last.then_inc(x2_ok, 1)

            def heads(post, late, mid, early):
                for h in range(H):
                    if mid and 1 <= h < H - 1:
                        maximum(mid, h + 1)
                    if early and isinstance(early.b, int) and early.b == 0:
                        for n in {2: ("wk", "wv"), 5: ("uw", "wo"), 7: ("u1", "v1")}.get(h, ()):
                            weight_low(n)
                        if h == 8:
                            for i in range(2):
                                dve.memset(ks[i][KR:P], 1.0).then_inc(const_ok, 1)
                    if post:
                        if h == 0:
                            norm_stats(1, post.b, x1, NT)
                        if h == 1:
                            norm_apply(1, post.b, x1, x1n, NT)
                        if h == 4:
                            low_part(chunks(6), x1T, x1T_h, x1T_l, post.b)
                        if h == 9:
                            post_mask(post, 6)
                        if h == 12:
                            post_sum(post)
                        if h == 14:
                            post_add(post, 7)
                    if late and not mid:
                        if h == 2:
                            ffn_stats(0)
                        if h == 3:
                            ffn_norm(0)
                        if h == 6:
                            ffn_turned(0, (0, 1))
                        if h == 7:
                            ffn_stats(1)
                        if h == 8:
                            ffn_norm(1)
                        if h == 14:
                            ffn_low(0)

            def between(post, late, mid, early):
                if late:
                    dve.wait_ge(max_read, H * (late.b + 1))
                    dve.tensor_scalar(smax_p[:, :, 0], smax[:], -1.0, None, ALU.mult).then_inc(msplit, 1)
                    dve.wait_ge(msplit, 3 * late.b + 1)
                    dve.scalar_tensor_tensor(out=smax_r[:], in0=smax[:], scalar=-1.0, in1=smax_p[:, :, 0], op0=ALU.mult, op1=ALU.subtract).then_inc(msplit, 1)
                    dve.wait_ge(msplit, 3 * late.b + 2)
                    dve.tensor_copy(smax_p[:, :, 1], smax_r[:]).then_inc(msplit, 1)
                    dve.wait_ge(msplit, 3 * late.b + 3)
                    dve.tensor_tensor(smax_p[:, :, 2], smax_r[:], smax_p[:, :, 1], ALU.subtract).then_inc(mparts, 1)
                if early:
                    if isinstance(early.b, int) and early.b <= 2:
                        dve.wait_ge(x_in[early.b], 16)
                    norm_stats(0, early.b, xres[:, early.b], NT)
                    if isinstance(early.b, int) and early.b == 0:
                        fill_buffers()
                if mid:
                    if isinstance(mid.b, int) and mid.b == 0:
                        dve.wait_ge(w_in["bv"], 16)
                    dve.wait_ge(qkv_ps["v"], mid.b + 1)
                    dve.tensor_tensor(vsb[mid.parity][:, :, :, 0:DH], bank[6][:, :].rearrange("p (t h w) -> p t h w", t=NT, w=DH),
                                      bv[:, None, :].to_broadcast([P, NT, D]).rearrange("p t (h w) -> p t h w", w=DH), ALU.add).then_inc(v_ok, 1)
                if post:
                    n = post.b
                    if isinstance(n, int) and n == 0:
                        dve.wait_ge(w_in["attention"], 16 * LOADS["attention"])
                    dve.wait_ge(cT_ps, n + 1)
                    dve.tensor_copy(cT[:], bank[7][:, 0:NC * SC].rearrange("p (c n) -> p c n", c=NC)).then_inc(cT_ok, 1)
                if early:
                    wait(dve, xT_ps, early.b)
                    norm_apply(0, early.b, xres[:, early.b], xn, NT)
                    if isinstance(early.b, int) and early.b == 0:
                        weight_low("wq")
                if post:
                    for t in range(NT):
                        rows = bank[2 + t][:, :].rearrange("p (h w) -> p h w", w=W)
                        dve.wait_ge(att_ps, NT * n + t + 1)
                        dve.reciprocal(att_rec[:, t], rows[:, :, DH]).then_inc(att_rc, 1)
                        dve.wait_ge(att_rc, NT * n + t + 1)
                        dve.tensor_tensor(att[:, t].rearrange("p (h w) -> p h w", w=DH), rows[:, :, 0:DH],
                                          att_rec[:, t, :, None].to_broadcast([P, H, DH]), ALU.mult).then_inc(att_ok, 1)
                    post_uq(post)
                    low_part(chunks(5), attT, attT_h, attT_l, n)
                if early:
                    low_part(chunks(6), xT, xT_h, xT_l, early.b)
                if mid:
                    for h in range(2):
                        maximum(mid, h)
                if post:
                    dve.wait_ge(proj_ps, n + 1)
                    dve.wait_ge(bo_added, n + 1)
                    dve.tensor_tensor(x1[:], xres[:, n], chunks(4), ALU.add).then_inc(x1_ok, 1)
                    dve.wait_ge(x1_ok, n + 1)

            def pair_of(i):
                return xres[:, bass.ds(2 * i, 2)].rearrange("p b t d -> p (b t) d")

            def ffn_stats(i):
                norm_stats(2, i, pair_of(i), FT)

            def ffn_norm(i):
                wait(dve, x2T_ps, NC * i)
                norm_apply(2, i, pair_of(i), x2n, FT)

            def ffn_turned(i, banks):
                for c in range(NC):
                    dve.wait_ge(x2T_h, NC * i + c + 1)
                    dve.tensor_tensor(x2T[1][:, c], bank[banks[c]][:, :], x2T[0][:, c].bitcast(F32), ALU.subtract).then_inc(x2T_l, 1)

            def ffn_low(i):
                dve.wait_ge(low_ps, i + 1)
                wait(dve, hid_ps, NF * i)
                dve.tensor_copy(low[:], bank[5][:, :]).then_inc(low_h, 1)
                dve.wait_ge(low_h, i + 1)
                dve.tensor_tensor(low[R:P], bank[5][R:P, :], low[R:P].bitcast(F32), ALU.subtract).then_inc(low_ok, 1)

            def ffn_out(i, half):
                dve.wait_ge(out_ps, 2 * i + half + 1)
                dve.wait_ge(b2_added, i + 1)
                y = xres[:, 2 * i + half]
                dve.tensor_tensor(y, y, chunks((4, 2)[half]), ALU.add).then_inc(y_ok, 1)

            def ffn(i, post, before, more):
                if post:
                    norm_stats(1, post.b, x1, NT)
                elif more:
                    ffn_stats(i + 1)
                if before:
                    ffn_out(i - 1, 0)
                if post:
                    norm_apply(1, post.b, x1, x1n, NT)
                elif more:
                    ffn_norm(i + 1)
                if before:
                    ffn_out(i - 1, 1)
                if more:
                    ffn_turned(i + 1, (6, 7))
                if post:
                    low_part(chunks(2), x1T, x1T_h, x1T_l, post.b)
                    post_mask(post, 2)
                if more:
                    ffn_low(i + 1)
                if post:
                    post_sum(post)
                dve.wait_ge(gel_used, NF // 2 * (i + 1))
                dve.tensor_copy(rank2[:], bank[3][:, :]).then_inc(r2_ok, 1)
                if post:
                    post_add(post, 6)
                    dve.wait_ge(x2_ok, B)

            steps(dve, between, heads, lambda post: ffn(0, post, False, True))
            with dve.Fori(1, PAIRS - 1) as i:
                ffn(i, None, True, True)
            ffn(PAIRS - 1, None, True, False)
            for half in range(2):
                ffn_out(PAIRS - 1, half)

        @block.scalar
        def _(act):
            for n in ("bq", "bk"):
                act.dma_start({"bq": bq, "bk": bk}[n][:], io[n]).then_inc(w_in[n], 16)
            act.dma_start(bv[:], io["bv"].partition_broadcast(P)).then_inc(w_in["bv"], 16)
            act.dma_start(bo[:], io["bo"].partition_broadcast(P)).then_inc(w_in["attention"], 16)
            act.dma_start(dpar[:], io["dpar"]).then_inc(w_in["attention"], 16)
            act.dma_start(mask_u8[:], io["mask"].partition_broadcast(P)).then_inc(w_in["attention"], 16)
            for i in range(2):
                act.dma_start(cbuf[i][:], io["ctx"][i]).then_inc(c_in[i], 16)

            def weight_high(n):
                act.wait_ge(w_in[n], 16 * LOADS.get(n, 1))
                act.activation(weights[n][1][:], weights[n][0][:], ACT.Copy).then_inc(w_high, 1)

            def high_part(ps, parts, ps_ok, high_ok, n):
                act.wait_ge(ps_ok, n + 1)
                act.activation(parts[0][:], ps, ACT.Copy).then_inc(high_ok, 1)

            def project_out(n, t, whole, parts, bias, e):
                act.wait_ge(qkv_ps[n], e.b + 1)
                if isinstance(e.b, int) and e.b == 0:
                    act.wait_ge(w_in["b" + n], 16)
                for c in range(NC):
                    last = act.activation(whole[:, c], chunks(t)[:, c], ACT.Identity, bias=bias[:, c:c + 1])
                last.then_inc(full[n], 1)
                for c in range(NC):
                    last = act.activation(parts[e.parity][:, 0, c], chunks(t)[:, c], ACT.Identity, bias=bias[:, c:c + 1])
                last.then_inc(part_h[n], 1)

            def middle_part(n, rest, parts, e):
                act.wait_ge(rest1[n], e.b + 1)
                act.activation(parts[e.parity][:, 1], rest[:], ACT.Copy).then_inc(part_m[n], 1)

            def softmax_head(s, h):
                g = h // HG
                if h % HG == 0 and g >= 2:
                    act.wait_ge(av_done, NG * s.b + g - 1)
                act.wait_ge(sc_ps, H * s.b + h + 1)
                act.activation(probs[g % 2][:, h % HG], chunks(2 + h % 2), ACT.Exp, scale=SCALE).then_inc(exp_done, 1)

            def copy_attention(s, half):
                act.wait_ge(av_done, NG * s.b + 2 * half + 2)
                act.activation(att_raw[:, 2 * half:2 * half + 2], chunks(4), ACT.Copy).then_inc(av_evac, 1)

            def post_exp(p):
                act.wait_ge(xs_neg, p.b + 1)
                for t in range(NT):
                    last = act.activation(xp[:, t], xsc[:, t], ACT.Exp, bias=xneg[:, t:t + 1], accum_out=xsum[:, t:t + 1])
                last.then_inc(xs_exp, 1)

            def post_up(p, t):
                act.wait_ge(up_ps, p.b + 1)
                act.activation(upT[:], chunks(t), ACT.Relu).then_inc(up_ok, 1)

            def post_xpT(p, t):
                act.wait_ge(xpT_ps, p.b + 1)
                act.activation(xpT[:], bank[t][0:SC, 0:S], ACT.Copy).then_inc(xpT_ok, 1)

            def heads(post, late, mid, early):
                for h in range(H):
                    if late:
                        softmax_head(late, h)
                        if h == 10:
                            copy_attention(late, 0)
                    if early:
                        if isinstance(early.b, int) and early.b == 0:
                            for n in {1: ("wk", "wv"), 5: ("uw", "wo"), 7: ("u1", "v1")}.get(h, ()):
                                weight_high(n)
                        if h == 2:
                            project_out("q", 5, qf, qp, bq, early)
                        if h == (7 if late else 3):
                            project_out("k", 7, kf, kp, bk, early)
                        if h == (6 if late else 4):
                            middle_part("q", qr, qp, early)
                        if h == (11 if late else 6):
                            middle_part("k", kr, kp, early)
                    if post:
                        if h == 3:
                            high_part(chunks(6), x1T, x1T_ps, x1T_h, post.b)
                        if h == 6:
                            post_up(post, 6)
                        if h == 10:
                            post_exp(post)
                        if h == 12:
                            post_xpT(post, 5)
                    if late and not mid and h == 5:
                        ffn_turned(0, (0, 1))

            def between(post, late, mid, early):
                if post:
                    copy_attention(post, 1)
                if late:
                    act.wait_ge(mT_ps, late.b + 1)
                    act.activation(smax_T[:], bank[5][0:3 * H, 0:S // 2].bitcast(BF16), ACT.Copy).then_inc(mT_ok, 1)
                    act.wait_ge(mT_ok, late.b + 1)
                    act.dma_start(qs[late.parity][KR:KM], smax_T[:]).then_inc(mstacked[late.parity], 16)
                if post:
                    high_part(chunks(5), attT, attT_ps, attT_h, post.b)
                if early:
                    if isinstance(early.b, int) and early.b == 0:
                        weight_high("wq")
                    high_part(chunks(6), xT, xT_ps, xT_h, early.b)

            def ffn_turned(i, banks):
                for c in range(NC):
                    act.wait_ge(x2T_ps, NC * i + c + 1)
                    act.activation(x2T[0][:, c], bank[banks[c]][:, :], ACT.Copy).then_inc(x2T_h, 1)

            def ffn(i, post, more):
                for f in range(NF):
                    act.wait_ge(hid_ps, NF * i + f + 1)
                    wait(act, gel_used, NF // 2 * i + (f - 4) // 2 + 1)
                    act.activation(gel[f % 4][:], bank[f % 2][:, :], ACT.Gelu_apprx_tanh, bias=b1[:, f:f + 1]).then_inc(gel_ok, 1)
                    if more and f == 3:
                        ffn_turned(i + 1, (6, 7))
                    if post and f == 3:
                        high_part(chunks(2), x1T, x1T_ps, x1T_h, post.b)
                    if post and f == 5:
                        post_up(post, 2)
                if post:
                    post_exp(post)
                    post_xpT(post, 7)

            def ffn_first(post):
                act.wait_ge(w_in["ffn"], 16 * LOADS["ffn"])
                ffn(0, post, True)

            steps(act, between, heads, ffn_first)
            with act.Fori(1, PAIRS - 1) as i:
                ffn(i, None, True)
            ffn(PAIRS - 1, None, False)

        @block.tensor
        def _(pe):
            pe.wait_ge(ident_ok, 4)
            parts_of = {n: (h, l) for n, (_, h, l) in weights.items()}

            def products(out, left, right, first=True, last=True):
                terms = ((0, 0), (0, 1), (1, 0))
                for n, (i, j) in enumerate(terms):
                    mm = pe.matmul(out, left[i], right[j], start=first and n == 0, stop=last and n == len(terms) - 1)
                return mm

            def to_channels(t, x, tiles):
                for c in range(NC):
                    for k in range(tiles):
                        last = pe.transpose(bank[t][:, c * S + k * P:c * S + (k + 1) * P], x[:, k, c * P:(c + 1) * P], ident[:])
                return last

            def project_rows(t, name, x):
                w = parts_of[name]
                for m in range(NC):
                    for c in range(NC):
                        last = products(chunks(t)[:, m], [w[i][:, c, m * P:(m + 1) * P] for i in range(2)], [x[i][:, c] for i in range(2)], c == 0, c == NC - 1)
                return last

            def project_tokens(t, name, x, tiles=range(NT)):
                w = parts_of[name]
                for k in tiles:
                    for c in range(NC):
                        last = products(chunks(t)[:, k], [x[i][:, c, k * P:(k + 1) * P] for i in range(2)], [w[i][:, c] for i in range(2)], c == 0, c == NC - 1)
                return last

            def max_scores(m, h):
                if h % (H // 2) == 0:
                    pe.wait_ge(stacked[m.parity][h // (H // 2)], 2 * NP * 16 * (m.turn + 1))
                if h >= 2:
                    pe.wait_ge(max_read, H * m.b + h - 1)
                for t in range(NT):
                    last = pe.matmul(chunks(h % 2)[:, t], qs[m.parity][0:KR, h, t * P:(t + 1) * P], ks[m.parity][0:KR, h], start=True, stop=True)
                last.then_inc(max_ps, 1)

            def scores(s, h):
                if h == 0:
                    pe.wait_ge(mstacked[s.parity], 16 * (s.turn + 1))
                if h >= 2:
                    pe.wait_ge(exp_done, H * s.b + h - 1)
                for t in range(NT):
                    last = pe.matmul(chunks(2 + h % 2)[:, t], ks[s.parity][0:KM, h, t * P:(t + 1) * P], qs[s.parity][0:KM, h], start=True, stop=True)
                last.then_inc(sc_ps, 1)

            def attend(s, g, post):
                if g == 0 and post:
                    pe.wait_ge(x1_ok, post.b + 1)
                if g == 2:
                    pe.wait_ge(av_evac, 2 * s.b + 1)
                pe.wait_ge(exp_done, H * s.b + HG * (g + 1))
                for t in range(NT):
                    for j in range(HG):
                        last = pe.matmul(chunks(4)[j * W:(j + 1) * W, g % 2], vsb[s.parity][:, t, HG * g + j], probs[g % 2][:, j, t],
                                         start=t == 0, stop=t == NT - 1, tile_position=(0, j * W))
                last.then_inc(av_done, 1)

            def post_x1T(p, t):
                pe.wait_ge(ln_done[1], p.b + 1)
                to_channels(t, x1n, NT).then_inc(x1T_ps, 1)

            def post_up(p, t):
                pe.wait_ge(x1T_l, p.b + 1)
                project_rows(t, "uw", x1T).then_inc(up_ps, 1)

            def post_xs(p, b):
                pe.wait_ge(uq_ok, p.b + 1)
                pe.wait_ge(up_ok, p.b + 1)
                for t in range(NT):
                    for c in range(NC):
                        last = pe.matmul(bank[b][:, t * SC:(t + 1) * SC], upT[:, c, t * P:(t + 1) * P], uqT[:, c], start=c == 0, stop=c == NC - 1)
                last.then_inc(xs_ps, 1)

            def post_xpT(p, b):
                pe.wait_ge(xs_exp, p.b + 1)
                for t in range(NT):
                    last = pe.transpose(bank[b][0:SC, t * P:(t + 1) * P], xp[:, t], ident[:])
                last.then_inc(xpT_ps, 1)

            def post_pv(p, b):
                pe.wait_ge(xpT_ok, p.b + 1)
                for t in range(NT):
                    last = pe.matmul(chunks(b)[:, t], xpT[:, t * P:(t + 1) * P], cbuf[p.parity][:], start=True, stop=True)
                last.then_inc(pv_ps, 1)

            def heads(post, late, mid, early):
                for h in range(H):
                    if early and h == 1:
                        pe.wait_ge(xT_l, early.b + 1)
                        if isinstance(early.b, int) and early.b == 0:
                            pe.wait_ge(w_low, 1)
                        if late and not post:
                            pe.wait_ge(mT_ok, late.b + 1)
                        project_rows(5, "wq", xT).then_inc(qkv_ps["q"], 1)
                    if mid and 1 <= h < H - 1:
                        max_scores(mid, h + 1)
                    if late and 1 <= h < H - 1:
                        scores(late, h + 1)
                    if late and h % HG == 1 and h > HG:
                        attend(late, h // HG - 1, post)
                    if early and h == (6 if late else 2):
                        if isinstance(early.b, int) and early.b == 0:
                            pe.wait_ge(w_low, 2)
                        project_rows(7, "wk", xT).then_inc(qkv_ps["k"], 1)
                    if post:
                        if h == 3:
                            post_x1T(post, 6)
                        if h == 5:
                            post_up(post, 6)
                        if h == 8:
                            post_xs(post, 6)
                        if h == 12:
                            if early:
                                pe.wait_ge(part_h["q"], early.b + 1)
                            post_xpT(post, 5)
                        if h == 14:
                            if early:
                                pe.wait_ge(part_h["k"], early.b + 1)
                            post_pv(post, 7)
                    if late and not mid:
                        if h == 4:
                            ffn_turn(0, (0, 1))
                        if h == 14:
                            low_rank(0)

            def between(post, late, mid, early):
                def values(tiles):
                    return project_tokens(6, "wv", xT, tiles)

                if mid:
                    if isinstance(mid.b, int) and mid.b == 0:
                        pe.wait_ge(w_low, 3)
                    values([0])
                if post:
                    n = post.b
                    attend(post, NG - 1, None)
                if late:
                    pe.wait_ge(mparts, late.b + 1)
                    if mid:
                        pe.wait_ge(part_h["q"], mid.b + 1)
                    for t in range(NT):
                        last = pe.transpose(bank[5][0:5 * H, t * P // 2:(t + 1) * P // 2].bitcast(BF16),
                                            smax_p[:, t].rearrange("p k h -> p (k h)"), ident_bf[:])
                    last.then_inc(mT_ps, 1)
                if post:
                    pe.wait_ge(c_in[post.parity], 16 * (post.turn + 1))
                    if mid:
                        pe.wait_ge(part_h["k"], mid.b + 1)
                    if not late:
                        pe.wait_ge(x2_ok, n)
                    for c in range(NC):
                        last = pe.transpose(bank[7][:, c * SC:(c + 1) * SC], cbuf[post.parity][:, c * P:(c + 1) * P], ident[0:SC, 0:SC])
                    last.then_inc(cT_ps, 1)
                if mid:
                    values([1]).then_inc(qkv_ps["v"], 1)
                if post:
                    pe.wait_ge(av_evac, 2 * n + 2)
                    for t in range(NT):
                        for g in range(NG):
                            last = pe.transpose(bank[2 + t][:, g * P:(g + 1) * P], att_raw[:, g, t * P:(t + 1) * P], ident[:])
                        last.then_inc(att_ps, 1)
                    pe.wait_ge(cT_ok, n + 1)
                    for m in range(NC):
                        for c in range(NC):
                            last = pe.matmul(bank[7][:, 256 + m * SC:256 + (m + 1) * SC], weights["uw"][0][:, c, m * P:(m + 1) * P], cT[:, c],
                                             start=c == 0, stop=c == NC - 1)
                    last.then_inc(uq_ps, 1)
                if mid:
                    for h in range(2):
                        max_scores(mid, h)
                if post:
                    pe.wait_ge(att_ok, NT * (n + 1))
                    if late:
                        pe.wait_ge(mT_ok, late.b + 1)
                    else:
                        pe.wait_ge(low_ok, 1)
                    to_channels(5, att, NT).then_inc(attT_ps, 1)
                if early:
                    pe.wait_ge(ln_done[0], early.b + 1)
                    if mid:
                        pe.wait_ge(v_ok, mid.b + 1)
                    to_channels(6, xn, NT).then_inc(xT_ps, 1)
                if late:
                    if isinstance(late.b, int) and late.b == 0:
                        pe.wait_ge(const_ok, 4)
                        pe.wait_ge(v_zero, 5)
                    for h in range(2):
                        scores(late, h)
                if post:
                    if isinstance(n, int) and n == 0:
                        pe.wait_ge(w_low, 5)
                    if not late:
                        hidden(0, 0)
                        hidden(0, 1)
                    pe.wait_ge(attT_l, n + 1)
                    project_tokens(4, "wo", attT).then_inc(proj_ps, 1)

            def ffn_turn(i, banks):
                pe.wait_ge(ln_done[2], i + 1)
                for c in range(NC):
                    for t in range(FT):
                        last = pe.transpose(bank[banks[c]][:, t * P:(t + 1) * P], x2n[:, t, c * P:(c + 1) * P], ident[:])
                    last.then_inc(x2T_ps, 1)

            def low_rank(i):
                pe.wait_ge(x2T_l, NC * (i + 1))
                if isinstance(i, int) and i == 0:
                    pe.wait_ge(w_low, len(weights))
                u1 = parts_of["u1"]
                for c in range(NC):
                    last = products(bank[5][:, :], [u1[k][:, c] for k in range(2)], [x2T[k][:, c] for k in range(2)], c == 0, c == NC - 1)
                last.then_inc(low_ps, 1)

            def hidden(i, f):
                if f == 0:
                    pe.wait_ge(low_ok, i + 1)
                wait(pe, gel_ok, NF * i + f - 1)
                for k in range(2):
                    last = pe.matmul(bank[f % 2][:, :], parts_of["v1"][k][:, f * P:(f + 1) * P], low[:], start=k == 0, stop=k == 1)
                last.then_inc(hid_ps, 1)

            def rank(i, f):
                pe.wait_ge(gel_ok, NF * i + f + 2)
                for k in range(2):
                    last = pe.matmul(bank[3][k * R:(k + 1) * R, :], u2[:, f + k], gel[(f + k) % 4][:], start=f == 0, stop=f == NF - 2,
                                     tile_position=(0, k * R))
                last.then_inc(gel_used, 1)

            def ffn(i, post, more):
                for f in range(0, NF, 2):
                    if post and f == 4:
                        post_xs(post, 2)
                    if f + 2 < NF:
                        hidden(i, f + 2)
                        hidden(i, f + 3)
                    rank(i, f)
                    if f == 0 and more:
                        ffn_turn(i + 1, (6, 7))
                    if f == 2:
                        if post:
                            post_x1T(post, 2)
                        if more:
                            low_rank(i + 1)
                        if post:
                            post_up(post, 2)
                if more:
                    hidden(i + 1, 0)
                    hidden(i + 1, 1)
                if post:
                    post_xpT(post, 7)
                pe.wait_ge(r2_ok, i + 1)
                for half in range(2):
                    if post and half == 1:
                        post_pv(post, 6)
                    for t in range(NT):
                        k = half * NT + t
                        last = pe.matmul(chunks((4, 2)[half])[:, t], rank2[:, k * P:(k + 1) * P], v2[:], start=True, stop=True)
                    last.then_inc(out_ps, 1)

            steps(pe, between, heads, lambda post: ffn(0, post, True))
            with pe.Fori(1, PAIRS - 1) as i:
                ffn(i, None, True)
            ffn(PAIRS - 1, None, False)


INS = ("x", "ctx", "mask", "wq", "wk", "wv", "wo", "uw", "bq", "bk", "bv", "bo", "dpar", "u1", "v1", "b1", "u2", "v2", "b2")


def kernel(x, ctx_1024, mask_BxS2_bf0, mask_BxS2_bk1, L0_attn_Wq, L0_attn_bq, L0_attn_Wk, L0_attn_bk, L0_attn_Wv, L0_attn_bv,
           L0_attn_Wo, L0_attn_bo, L0_xattn_U_w, L0_xattn_D_param, L0_ffn_U1, L0_ffn_V1, L0_ffn_b1, L0_ffn_U2, L0_ffn_V2, L0_ffn_b2):
    import concourse.bacc as bacc
    from concourse.bass_utils import run_bass_kernel_spmd

    heads, D = 16, x.shape[-1]
    chunks, dh = D // P, D // heads

    def head_minor(w):
        w = np.asarray(w)
        w4 = w.reshape(2, heads // 2 // chunks, chunks, dh, *w.shape[1:])
        return np.transpose(w4, (2, 0, 3, 1, *range(4, w4.ndim))).reshape(w.shape)

    def columns(v):
        return np.asarray(v).reshape(-1, P).T

    laid = {
        "x": x, "ctx": ctx_1024, "mask": mask_BxS2_bk1,
        "wq": head_minor(L0_attn_Wq).T, "wk": head_minor(L0_attn_Wk).T, "wv": np.asarray(L0_attn_Wv).T, "wo": np.asarray(L0_attn_Wo).T,
        "uw": np.asarray(L0_xattn_U_w).T, "bq": columns(head_minor(L0_attn_bq)), "bk": columns(head_minor(L0_attn_bk)),
        "bv": L0_attn_bv, "bo": L0_attn_bo, "dpar": columns(L0_xattn_D_param), "u1": L0_ffn_U1, "v1": L0_ffn_V1,
        "b1": columns(L0_ffn_b1), "u2": L0_ffn_U2, "v2": L0_ffn_V2, "b2": L0_ffn_b2,
    }
    nc = bacc.Bacc("TRN2", target_bir_lowering=False, num_devices=1)
    arrays, io = {}, {}
    for name in INS:
        a = np.ascontiguousarray(laid[name])
        arrays[f"in_{name}"] = a
        io[name] = nc.dram_tensor(f"in_{name}", a.shape, mybir.dt.from_np(a.dtype), kind="ExternalInput").ap()
    io["out"] = nc.dram_tensor("out_y", x.shape, F32, kind="ExternalOutput").ap()
    decoder_layer(nc, io)
    return run_bass_kernel_spmd(nc, [arrays], core_ids=[0]).results[0]["out_y"]
```

```python
from contextlib import ExitStack

import numpy as np
import concourse.bass as bass
from concourse import mybir

ALU = mybir.AluOpType
ACT = mybir.ActivationFunctionType
AX = mybir.AxisListType
F32 = mybir.dt.float32
F32R = mybir.dt.float32r
BF16 = mybir.dt.bfloat16
U8 = mybir.dt.uint8

P = 128
EPS = 1e-5
MASKED = -3.0e38
ONES = float(np.uint32(0x3F803F80).view(np.float32))
Q_PARTS = (0, 0, 0, 1, 1, 2)
K_PARTS = (0, 1, 2, 0, 1, 0)


class Batch:

    def __init__(self, b, parity, turn):
        self.b, self.parity, self.turn = b, parity, turn


def batch_at(pair, k):
    return Batch(2 * pair + k, k % 2, pair + k // 2)


def decoder_layer(nc, io):
    B, S, D = io["x"].shape
    SC = io["ctx"].shape[1]
    NT, NC = S // P, D // P
    H, DH = 16, D // 16
    HC = H // NC
    HG = 4
    NG = H // HG
    W = 32
    F = io["b1"].shape[0] * io["b1"].shape[1]
    NF = F // P
    R = io["u1"].shape[-1]
    NP = len(Q_PARTS)
    KR = NP * DH
    KM = KR + 3
    SCALE = float(DH) ** -0.5
    FT = 2 * NT
    FN = FT * P
    LOADS = {"u1": 2, "v1": 2, "attention": 3, "ffn": 5}
    assert S == 2 * P and D == 2 * P and R == 64 and H % HG == 0 and B % 2 == 0

    ctx = ExitStack()
    with ctx:
        def sb(name, shape, dt=F32):
            return ctx.enter_context(nc.sbuf_tensor(name, shape, dt))

        def sem(name):
            return ctx.enter_context(nc.semaphore(name))

        ident = sb("ident", [P, P])
        ident_bf = sb("ident_bf", [P, P], BF16)
        weights = {}
        for n, cols in (("wk", D), ("wq", D), ("wv", D), ("uw", D), ("wo", D), ("u1", P)):
            weights[n] = (sb(n + "_f", [P, NC, cols]), sb(n + "_h", [P, NC, cols], F32R), sb(n + "_l", [P, NC, cols], F32R))
        weights["v1"] = (sb("v1_f", [P, F]), sb("v1_h", [P, F], F32R), sb("v1_l", [P, F], F32R))
        u2 = sb("u2", [P, NF, R])
        v2 = sb("v2", [P, D])
        bq, bk, dpar = sb("bq_sb", [P, NC]), sb("bk_sb", [P, NC]), sb("dpar_sb", [P, NC])
        b1 = sb("b1_sb", [P, NF])
        bv, bo, b2 = sb("bv_sb", [P, D]), sb("bo_sb", [P, D]), sb("b2_sb", [P, D])
        mask_u8 = sb("mask_u8", [P, B, SC], U8)
        neg_mask = sb("neg_mask", [P, SC])
        wait_pad = sb("wait_pad", [P, 1])
        minus_half, eps_sb = sb("minus_half", [P, FT]), sb("eps", [P, FT])

        xres = sb("xres", [P, B, NT, D])
        cbuf = [sb(f"cbuf{i}", [SC, D]) for i in range(2)]
        stats = [sb(f"stats{i}", [P, FT, 6]) for i in range(3)]
        mv = [sb(f"mv{i}", [P, FT, 2]) for i in range(3)]
        var_eps = [sb(f"var_eps{i}", [P, FT]) for i in range(3)]
        rstd = [sb(f"rstd{i}", [P, FT]) for i in range(3)]
        xn = sb("xn", [P, NT, D])
        xT = (sb("xT_h", [P, NC, S], F32R), sb("xT_l", [P, NC, S], F32R))
        qf, kf = sb("qf", [P, NC, S]), sb("kf", [P, NC, S])
        qr, kr = sb("qr", [P, NC, S]), sb("kr", [P, NC, S])
        qp = [sb(f"qp{i}", [P, 3, NC, S], BF16) for i in range(2)]
        kp = [sb(f"kp{i}", [P, 3, NC, S], BF16) for i in range(2)]
        qs = [sb(f"qs{i}", [P, H, S], BF16) for i in range(2)]
        ks = [sb(f"ks{i}", [P, H, S], BF16) for i in range(2)]
        vsb = [sb(f"v{i}", [P, NT, H, W]) for i in range(2)]
        smax = sb("smax", [P, NT, H])
        smax_r = sb("smax_r", [P, NT, H])
        smax_p = sb("smax_p", [P, NT, 5, H], BF16)
        smax_T = sb("smax_T", [3 * H, S], BF16)
        probs = [sb(f"probs{i}", [P, HG, NT, S]) for i in range(2)]
        att_raw = sb("att_raw", [P, NG, S])
        att_rec = sb("att_rec", [P, NT, H])
        att = sb("att", [P, NT, D])
        attT = (sb("attT_h", [P, NC, S], F32R), sb("attT_l", [P, NC, S], F32R))
        x1 = sb("x1", [P, NT, D])
        x1n = sb("x1n", [P, NT, D])
        x1T = (sb("x1T_h", [P, NC, S], F32R), sb("x1T_l", [P, NC, S], F32R))
        cT = sb("cT", [P, NC, SC])
        upT = sb("upT", [P, NC, S])
        uqT = sb("uqT", [P, NC, SC])
        xsc = sb("xsc", [P, NT, SC])
        xmax, xneg, xsum, xrec = (sb(n, [P, NT]) for n in ("xmax", "xneg", "xsum", "xrec"))
        xp = sb("xp", [P, NT, SC])
        xpT = sb("xpT", [SC, S])
        x2n = sb("x2n", [P, FT, D])
        x2T = (sb("x2T_h", [P, NC, FN], F32R), sb("x2T_l", [P, NC, FN], F32R))
        low = sb("low", [P, FN], F32R)
        gel = [sb(f"gel{i}", [P, FN]) for i in range(4)]
        rank2 = sb("rank2", [P, FN])

        bank = [ctx.enter_context(nc.psum_tensor(f"bank{i}", [P, 512], F32)) for i in range(8)]

        def chunks(t):
            return bank[t][:, :].rearrange("p (c n) -> p c n", c=2)

        w_in = {n: sem(n + "_loaded") for n in (*weights, "bq", "bk", "bv", "attention", "ffn")}
        x_in, c_in = [sem(f"x_loaded{i}") for i in range(4)], [sem(f"ctx_loaded{i}") for i in range(2)]
        v_zero = sem("buffers_zeroed")
        ident_ok, const_ok, w_high, w_low, w_low_later = sem("ident_ok"), sem("const_ok"), sem("w_high"), sem("w_low"), sem("w_low_later")
        ln_stats, ln_mv, ln_var, ln_rstd, ln_done = ([sem(f"{n}{i}") for i in range(3)] for n in ("ln_stats", "ln_mv", "ln_var", "ln_rstd", "ln_done"))
        xT_ps, xT_h, xT_l = sem("xT_in_psum"), sem("xT_high"), sem("xT_low")
        qkv_ps = {n: sem(n + "_in_psum") for n in "qkv"}
        full = {n: sem(n + "_full") for n in "qk"}
        part_h, part_m, part_l = ({n: sem(f"{n}_part_{p}") for n in "qk"} for p in "hml")
        rest1 = {n: sem(n + "_rest") for n in "qk"}
        v_ok = sem("v_ready")
        stacked = [[sem(f"stacked{i}_heads{j}") for j in range(2)] for i in range(2)]
        mstacked = [sem(f"max_stacked{i}") for i in range(2)]
        max_ps, max_read = sem("max_scores_in_psum"), sem("max_scores_read")
        msplit, mparts, mT_ps, mT_ok = sem("max_split_step"), sem("max_parts"), sem("maxT_in_psum"), sem("maxT_ready")
        sc_ps, exp_done, av_done, av_evac = sem("scores_in_psum"), sem("probs_ready"), sem("av_group_done"), sem("av_copied")
        att_ps, att_rc, att_ok = sem("att_in_psum"), sem("att_reciprocal"), sem("att_normed")
        attT_ps, attT_h, attT_l = sem("attT_in_psum"), sem("attT_high"), sem("attT_low")
        bo_added, proj_ps, x1_ok = sem("bo_added"), sem("proj_in_psum"), sem("x1_ready")
        x1T_ps, x1T_h, x1T_l = sem("x1T_in_psum"), sem("x1T_high"), sem("x1T_low")
        cT_ps, cT_ok, uq_ps, uq_ok, up_ps, up_ok = (sem(n) for n in ("cT_in_psum", "cT_ready", "uq_in_psum", "uq_ready", "up_in_psum", "up_ready"))
        mask_ok = sem("mask_ok")
        xs_ps, xs_max, xs_neg, xs_exp, xs_rec = (sem(n) for n in ("xs_in_psum", "xs_masked", "xs_negmax", "xs_exp", "xs_reciprocal"))
        xpT_ps, xpT_ok, pv_ps, x2_ok = (sem(n) for n in ("xpT_in_psum", "xpT_ready", "pv_in_psum", "x2_ready"))
        x2T_ps, x2T_h, x2T_l = sem("x2T_in_psum"), sem("x2T_high"), sem("x2T_low")
        low_ps, low_h, low_ok = sem("low_in_psum"), sem("low_high"), sem("low_ready")
        hid_ps, gel_ok, gel_used, r2_ok = (sem(n) for n in ("hidden_in_psum", "gelu_ready", "gelu_used", "rank2_ready"))
        out_ps, b2_added, y_ok, stored = sem("ffn_in_psum"), sem("b2_added"), sem("y_ready"), sem("stored")

        def wait(eng, s, n):
            if not (isinstance(n, int) and n <= 0):
                eng.wait_ge(s, n)

        def place(h):
            return h % HC * NC + h // HC

        PAIRS = B // 2
        block = ctx.enter_context(nc.Block())

        def steps(eng, between, heads):
            def at(b):
                return [batch_at(0, b + d) if 0 <= b + d < B else None for d in range(4)]

            for b in range(-3, 0):
                between(*at(b))
                heads(*at(b))
            whole = (B - 3) // 2
            with eng.Fori(0, whole) as pair:
                for k in range(2):
                    now = [batch_at(pair, k + d) for d in range(4)]
                    between(*now)
                    heads(*now)
            for b in range(2 * whole, B - 1):
                between(*at(b))
                heads(*at(b))
            between(*at(B - 1))

        @block.sync
        def _(sp):
            sp.dma_start(xres[:, 0:1], io["x"][0:1].rearrange("b (t p) d -> p b t d", p=P)).then_inc(x_in[0], 16)
            for n in ("wk", "wq", "wv"):
                sp.dma_start(weights[n][0][:], io[n].rearrange("(c p) n -> p c n", p=P)).then_inc(w_in[n], 16)
            sp.dma_start(xres[:, 1:2], io["x"][1:2].rearrange("b (t p) d -> p b t d", p=P)).then_inc(x_in[1], 16)
            sp.dma_start(xres[:, 2:3], io["x"][2:3].rearrange("b (t p) d -> p b t d", p=P)).then_inc(x_in[2], 16)
            for n in ("uw", "wo"):
                sp.dma_start(weights[n][0][:], io[n].rearrange("(c p) n -> p c n", p=P)).then_inc(w_in[n], 16)
            for n, t in (("bo", bo), ("mask", mask_u8)):
                sp.dma_start(t[:], io[n].partition_broadcast(P)).then_inc(w_in["attention"], 16)
            sp.dma_start(dpar[:], io["dpar"]).then_inc(w_in["attention"], 16)
            for i in range(2):
                sp.dma_start(cbuf[i][:], io["ctx"][i]).then_inc(c_in[i], 16)

            def load_rest():
                sp.dma_start(xres[:, 3:B], io["x"][3:B].rearrange("b (t p) d -> p b t d", p=P)).then_inc(x_in[3], 16)
                for half in range(2):
                    sp.dma_start(weights["u1"][0][:, :, half * R:(half + 1) * R], io["u1"].rearrange("(c p) n -> p c n", p=P)).then_inc(w_in["u1"], 16)
                    sp.dma_start(weights["v1"][0][half * R:(half + 1) * R, :], io["v1"]).then_inc(w_in["v1"], 16)
                    sp.dma_start(v2[half * R:(half + 1) * R, :], io["v2"]).then_inc(w_in["ffn"], 16)
                sp.dma_start(u2[:], io["u2"].rearrange("(f p) n -> p f n", p=P)).then_inc(w_in["ffn"], 16)
                sp.dma_start(b1[:], io["b1"]).then_inc(w_in["ffn"], 16)
                sp.dma_start(b2[:], io["b2"].partition_broadcast(P)).then_inc(w_in["ffn"], 16)

            cuts = (("k", 0, part_h), ("q", 0, part_h), ("q", 1, part_m), ("q", 2, part_l), ("k", 1, part_m), ("k", 2, part_l))
            stacks = {"q": (qp, Q_PARTS, qs), "k": (kp, K_PARTS, ks)}

            def stack(e, half):
                for n, level, done in cuts:
                    parts, which, dst = stacks[n]
                    if half != 1:
                        sp.wait_ge(done[n], e.b + 1)
                    for row in (i for i, w in enumerate(which) if w == level):
                        rows, part = dst[e.parity][row * DH:(row + 1) * DH], parts[e.parity][:, level]
                        if half is None:
                            sp.dma_start(rows.rearrange("r (h c) s -> r h (c s)", c=NC), part.rearrange("p c s -> p (c s)")).then_inc(stacked[e.parity][1], 16)
                        else:
                            sp.dma_start(rows.rearrange("r (h c) s -> r h c s", c=NC)[:, :, half], part[:, half]).then_inc(stacked[e.parity][half], 16)

            def heads(post, late, mid, early):
                if early:
                    stack(early, 0 if late else None)
                    if isinstance(early.b, int) and early.b == 1:
                        load_rest()
                if post and mid:
                    sp.wait_ge(pv_ps, post.b + 1)
                    sp.dma_start(cbuf[mid.parity][:], io["ctx"][mid.b]).then_inc(c_in[mid.parity], 16)

            def between(post, late, mid, early):
                if mid and post:
                    sp.wait_ge(sc_ps, H * (post.b + 1))
                    stack(mid, 1)

            steps(sp, between, heads)

            def store(b):
                sp.wait_ge(y_ok, b + 1)
                sp.dma_start(io["out"][bass.ds(b, 1)].rearrange("b (t p) d -> p b t d", p=P), xres[:, bass.ds(b, 1)]).then_inc(stored, 16)

            with sp.Fori(0, B) as b:
                store(b)
            sp.wait_ge(stored, 16 * B)

        @block.gpsimd
        def _(pool):
            pool.memset(ident[:], 0.0).then_inc(ident_ok, 1)
            pool.memset(ident_bf[:], 0.0).then_inc(ident_ok, 1)
            pool.memset(minus_half[:], -0.5).then_inc(const_ok, 1)
            pool.memset(eps_sb[:], EPS).then_inc(const_ok, 1)
            pool.wait_ge(ident_ok, 2)
            for m in (ident, ident_bf):
                pool.affine_select(out=m[:], in_=m[:], compare_op=ALU.not_equal, fill=1.0, base=0,
                                   pattern=[[-1, P]], channel_multiplier=1).then_inc(ident_ok, 1)
            pool.wait_ge(const_ok, 2)
            pool.wait_ge(ident_ok, 4)

            def rstd_of(ln, n, tiles):
                pool.wait_ge(ln_mv[ln], n + 1)
                pool.tensor_tensor(var_eps[ln][:, 0:tiles], mv[ln][:, 0:tiles, 1], eps_sb[:, 0:tiles], ALU.add).then_inc(ln_var[ln], 1)
                pool.wait_ge(ln_var[ln], n + 1)
                pool.tensor_tensor(rstd[ln][:, 0:tiles], var_eps[ln][:, 0:tiles], minus_half[:, 0:tiles], ALU.pow).then_inc(ln_rstd[ln], 1)

            def cut(n, whole, rest, parts, e, low_part):
                if not low_part:
                    if isinstance(e.b, int) and e.b == 1:
                        pool.wait_ge(part_l[n], e.b)
                    pool.wait_ge(full[n], e.b + 1)
                    pool.wait_ge(part_h[n], e.b + 1)
                    pool.tensor_tensor(rest[:], whole[:], parts[e.parity][:, 0], ALU.subtract).then_inc(rest1[n], 1)
                else:
                    pool.wait_ge(part_m[n], e.b + 1)
                    pool.tensor_tensor(parts[e.parity][:, 2], rest[:], parts[e.parity][:, 1], ALU.subtract).then_inc(part_l[n], 1)

            def heads(post, late, mid, early):
                if post:
                    rstd_of(1, post.b, NT)
                if late:
                    if isinstance(late.b, int) and late.b == 0:
                        pool.wait_ge(w_in["attention"], 16 * LOADS["attention"])
                    pool.wait_ge(ln_done[0], late.b + 1)
                    pool.tensor_tensor(xres[:, late.b], xres[:, late.b], bo[:, None, :].to_broadcast([P, NT, D]), ALU.add).then_inc(bo_added, 1)
                if early:
                    if isinstance(early.b, int) and early.b == 0:
                        rstd_of(0, 1, NT)
                    q_cut, k_cut = ("q", qf, qr, qp, early), ("k", kf, kr, kp, early)
                    if late:
                        order = ((q_cut, False), (q_cut, True), (k_cut, False), (k_cut, True))
                    else:
                        order = ((k_cut, False), (q_cut, False), (k_cut, True), (q_cut, True))
                    for what, low_part in order:
                        cut(*what, low_part)
                    if isinstance(early.b, int) and early.b in (1, 2):
                        for n in {1: ("uw", "wo"), 2: ("u1", "v1")}[early.b]:
                            whole, high, lo = weights[n]
                            pool.wait_ge(w_high, tuple(weights).index(n) + 1)
                            pool.tensor_tensor(lo[:], whole[:], high[:].bitcast(F32), ALU.subtract).then_inc(w_low_later, 1)
                if mid and not early:
                    rstd_of(2, 0, FT)
                if late and not mid:
                    rstd_of(2, 1, FT)

            def between(post, late, mid, early):
                if early and not (isinstance(early.b, int) and early.b == 1):
                    rstd_of(0, early.b, NT)

            def ffn(i, post):
                if post:
                    rstd_of(1, post.b, NT)
                if i + 2 < PAIRS:
                    rstd_of(2, i + 2, FT)
                pool.wait_ge(ln_done[2], i + 1)
                pair = xres[:, 2 * i:2 * i + 2].rearrange("p b t d -> p (b t) d")
                pool.tensor_tensor(pair, pair, b2[:, None, :].to_broadcast([P, FT, D]), ALU.add).then_inc(b2_added, 1)

            steps(pool, between, heads)
            pool.wait_ge(w_in["ffn"], 16 * LOADS["ffn"])
            for i in range(PAIRS):
                ffn(i, batch_at(0, B - 1) if i == 0 else None)

        @block.vector
        def _(dve):
            for i in range(2):
                dve.memset(vsb[i][:], 0.0).then_inc(v_zero, 1)
            dve.memset(smax_p[:], 0.0).then_inc(v_zero, 1)
            dve.wait_ge(v_zero, 3)
            for i in range(2):
                dve.memset(vsb[i][:, :, :, DH:DH + 1], 1.0).then_inc(v_zero, 1)

            def weight_low(n):
                whole, high, lo = weights[n]
                dve.wait_ge(w_high, tuple(weights).index(n) + 1)
                dve.tensor_tensor(lo[:], whole[:], high[:].bitcast(F32), ALU.subtract).then_inc(w_low, 1)

            def norm_stats(ln, n, x, tiles):
                for t in range(tiles):
                    last = dve.bn_stats(stats[ln][:, t], x[:, t])
                last.then_inc(ln_stats[ln], 1)
                dve.wait_ge(ln_stats[ln], n + 1)
                dve.memset(wait_pad[:], 0.0)
                for t in range(tiles):
                    last = dve.bn_aggr(mv[ln][:, t], stats[ln][:, t])
                last.then_inc(ln_mv[ln], 1)

            def norm_apply(ln, n, x, y, tiles):
                dve.wait_ge(ln_rstd[ln], n + 1)
                for t in range(tiles):
                    last = dve.tensor_scalar(y[:, t], x[:, t], mv[ln][:, t, 0:1], rstd[ln][:, t:t + 1], ALU.subtract, ALU.mult)
                last.then_inc(ln_done[ln], 1)

            def low_part(ps, parts, high_ok, lo_ok, n):
                dve.wait_ge(high_ok, n + 1)
                dve.tensor_tensor(parts[1][:], ps, parts[0][:].bitcast(F32), ALU.subtract).then_inc(lo_ok, 1)

            def maximum(m, h):
                dve.wait_ge(max_ps, H * m.b + h + 1)
                dve.tensor_reduce(smax[:, :, place(h)], chunks(h % 2), AX.X, ALU.max).then_inc(max_read, 1)

            def post_uq(p):
                dve.wait_ge(uq_ps, p.b + 1)
                for c in range(NC):
                    last = dve.tensor_scalar(uqT[:, c], bank[7][:, 256 + c * SC:256 + (c + 1) * SC], 0.0, dpar[:, c:c + 1], ALU.max, ALU.mult)
                last.then_inc(uq_ok, 1)

            def post_mask(p, scores):
                dve.wait_ge(xs_ps, p.b + 1)
                dve.tensor_scalar(neg_mask[:], mask_u8[:, p.b], MASKED, None, ALU.mult).then_inc(mask_ok, 1)
                dve.wait_ge(mask_ok, p.b + 1)
                dve.memset(wait_pad[:], 0.0)
                for t in range(NT):
                    last = dve.tensor_tensor_reduce(xsc[:, t], bank[scores][:, t * SC:(t + 1) * SC], neg_mask[:], 1.0, MASKED,
                                                    ALU.add, ALU.max, xmax[:, t:t + 1])
                last.then_inc(xs_max, 1)
                dve.wait_ge(xs_max, p.b + 1)
                dve.tensor_scalar(xneg[:], xmax[:], 4.0, -0.25, ALU.mult, ALU.mult).then_inc(xs_neg, 1)

            def post_sum(p):
                dve.wait_ge(xs_exp, p.b + 1)
                dve.reciprocal(xrec[:], xsum[:]).then_inc(xs_rec, 1)

            def post_add(p, values):
                dve.wait_ge(xs_rec, p.b + 1)
                dve.wait_ge(pv_ps, p.b + 1)
                for t in range(NT):
                    last = dve.scalar_tensor_tensor(out=xres[:, p.b, t], in0=bank[values][:, t * D:(t + 1) * D], scalar=xrec[:, t:t + 1],
                                                    in1=x1[:, t], op0=ALU.mult, op1=ALU.add)
                last.then_inc(x2_ok, 1)

            def early_stats(e):
                if isinstance(e.b, int) and e.b <= 2:
                    dve.wait_ge(x_in[e.b], 16)
                norm_stats(0, e.b, xres[:, e.b], NT)

            def heads(post, late, mid, early):
                if early and isinstance(early.b, int) and early.b == 0:
                    for n in ("wq", "wv"):
                        weight_low(n)
                    early_stats(batch_at(0, 1))
                    for i in range(2):
                        dve.memset(ks[i][KR:P].bitcast(F32), ONES).then_inc(const_ok, 1)
                if mid and not late:
                    for h in range(2):
                        maximum(mid, h)
                if late and not post:
                    dve.wait_ge(x_in[3], 16)
                for h in range(H):
                    if mid and 1 <= h < H - 1:
                        maximum(mid, h + 1)
                    if early and late and h == 10:
                        dve.wait_ge(rest1["k"], early.b + 1)
                        dve.tensor_copy(kp[early.parity][:, 1], kr[:]).then_inc(part_m["k"], 1)
                    if post:
                        if h == 0:
                            norm_stats(1, post.b, x1, NT)
                        if h == 2:
                            norm_apply(1, post.b, x1, x1n, NT)
                        if h == 5:
                            low_part(chunks(6), x1T, x1T_h, x1T_l, post.b)
                        if h == 9:
                            post_mask(post, 6)
                        if h == 12:
                            post_sum(post)
                        if h == 14:
                            post_add(post, 7)
                    if mid and not early:
                        if h == 3:
                            ffn_stats(0)
                        if h == 6:
                            ffn_norm(0)
                    if late and not mid:
                        if h == 3:
                            ffn_low(0)
                        if h == 9:
                            ffn_stats(1)
                        if h == 12:
                            ffn_norm(1)

            def between(post, late, mid, early):
                if late:
                    dve.wait_ge(max_read, H * (late.b + 1))
                    dve.tensor_scalar(smax_p[:, :, 0], smax[:], -1.0, None, ALU.mult).then_inc(msplit, 1)
                    dve.wait_ge(msplit, 3 * late.b + 1)
                    dve.scalar_tensor_tensor(out=smax_r[:], in0=smax[:], scalar=-1.0, in1=smax_p[:, :, 0], op0=ALU.mult, op1=ALU.subtract).then_inc(msplit, 1)
                    dve.wait_ge(msplit, 3 * late.b + 2)
                    dve.tensor_copy(smax_p[:, :, 1], smax_r[:]).then_inc(msplit, 1)
                    dve.wait_ge(msplit, 3 * late.b + 3)
                    dve.tensor_tensor(smax_p[:, :, 2], smax_r[:], smax_p[:, :, 1], ALU.subtract).then_inc(mparts, 1)
                if early:
                    if not (isinstance(early.b, int) and early.b == 1):
                        early_stats(early)
                if post:
                    n = post.b
                    if isinstance(n, int) and n == 0:
                        dve.wait_ge(w_in["attention"], 16 * LOADS["attention"])
                if mid:
                    if isinstance(mid.b, int) and mid.b == 0:
                        dve.wait_ge(w_in["bv"], 16)
                    dve.wait_ge(qkv_ps["v"], mid.b + 1)
                    dve.tensor_tensor(vsb[mid.parity][:, :, :, 0:DH], bank[6][:, :].rearrange("p (t h w) -> p t h w", t=NT, w=DH),
                                      bv[:, None, :].to_broadcast([P, NT, D]).rearrange("p t (h w) -> p t h w", w=DH), ALU.add).then_inc(v_ok, 1)
                if post:
                    dve.wait_ge(cT_ps, n + 1)
                    dve.tensor_copy(cT[:], bank[7][:, 0:NC * SC].rearrange("p (c n) -> p c n", c=NC)).then_inc(cT_ok, 1)
                    for t in range(NT):
                        rows = bank[2 + t][:, :].rearrange("p (h w) -> p h w", w=W)
                        dve.wait_ge(att_ps, NT * n + t + 1)
                        dve.reciprocal(att_rec[:, t], rows[:, :, DH]).then_inc(att_rc, 1)
                        dve.wait_ge(att_rc, NT * n + t + 1)
                        dve.tensor_tensor(att[:, t].rearrange("p (h w) -> p h w", w=DH), rows[:, :, 0:DH],
                                          att_rec[:, t, :, None].to_broadcast([P, H, DH]), ALU.mult).then_inc(att_ok, 1)
                if early:
                    wait(dve, xT_ps, early.b)
                    norm_apply(0, early.b, xres[:, early.b], xn, NT)
                    if isinstance(early.b, int) and early.b == 0:
                        weight_low("wk")
                if post:
                    low_part(chunks(5), attT, attT_h, attT_l, n)
                if early:
                    low_part(chunks(6), xT, xT_h, xT_l, early.b)
                if late and not mid:
                    ffn_turned(0, (0, 1))
                if post:
                    post_uq(post)
                if mid and late:
                    for h in range(2):
                        maximum(mid, h)
                if post:
                    dve.wait_ge(proj_ps, n + 1)
                    dve.wait_ge(bo_added, n + 1)
                    dve.tensor_tensor(x1[:], xres[:, n], chunks(4), ALU.add).then_inc(x1_ok, 1)
                    dve.wait_ge(x1_ok, n + 1)

            def pair_of(i):
                return xres[:, 2 * i:2 * i + 2].rearrange("p b t d -> p (b t) d")

            def ffn_stats(i):
                norm_stats(2, i, pair_of(i), FT)

            def ffn_norm(i):
                wait(dve, x2T_ps, NC * i)
                norm_apply(2, i, pair_of(i), x2n, FT)

            def ffn_turned(i, banks):
                for c in range(NC):
                    dve.wait_ge(x2T_h, NC * i + c + 1)
                    dve.tensor_tensor(x2T[1][:, c], bank[banks[c]][:, :], x2T[0][:, c].bitcast(F32), ALU.subtract).then_inc(x2T_l, 1)

            def ffn_low(i):
                dve.wait_ge(low_ps, i + 1)
                wait(dve, hid_ps, NF * i)
                dve.tensor_copy(low[:], bank[5][:, :]).then_inc(low_h, 1)
                dve.wait_ge(low_h, i + 1)
                dve.tensor_tensor(low[R:P], bank[5][R:P, :], low[R:P].bitcast(F32), ALU.subtract).then_inc(low_ok, 1)

            def ffn_out(i, half):
                dve.wait_ge(out_ps, 2 * i + half + 1)
                dve.wait_ge(b2_added, i + 1)
                y = xres[:, 2 * i + half]
                dve.tensor_tensor(y, y, chunks((4, 2)[half]), ALU.add).then_inc(y_ok, 1)

            def ffn(i, post):
                if post:
                    norm_stats(1, post.b, x1, NT)
                    norm_apply(1, post.b, x1, x1n, NT)
                if i > 0:
                    for half in range(2):
                        ffn_out(i - 1, half)
                if i + 1 < PAIRS:
                    ffn_turned(i + 1, (6, 7))
                if post:
                    low_part(chunks(2), x1T, x1T_h, x1T_l, post.b)
                if i + 2 < PAIRS:
                    ffn_stats(i + 2)
                if i + 1 < PAIRS:
                    ffn_low(i + 1)
                if post:
                    post_mask(post, 2)
                    post_sum(post)
                dve.wait_ge(gel_used, NF // 2 * (i + 1))
                dve.tensor_copy(rank2[:], bank[3][:, :]).then_inc(r2_ok, 1)
                if i + 2 < PAIRS:
                    ffn_norm(i + 2)
                if post:
                    post_add(post, 5)
                    dve.wait_ge(x2_ok, B)

            steps(dve, between, heads)
            for i in range(PAIRS):
                ffn(i, batch_at(0, B - 1) if i == 0 else None)
            for half in range(2):
                ffn_out(PAIRS - 1, half)

        @block.scalar
        def _(act):
            for n in ("bk", "bq"):
                act.dma_start({"bq": bq, "bk": bk}[n][:], io[n]).then_inc(w_in[n], 16)
            act.dma_start(bv[:], io["bv"].partition_broadcast(P)).then_inc(w_in["bv"], 16)

            def weight_high(n):
                act.wait_ge(w_in[n], 16 * LOADS.get(n, 1))
                act.activation(weights[n][1][:], weights[n][0][:], ACT.Copy).then_inc(w_high, 1)

            def high_part(ps, parts, ps_ok, high_ok, n):
                act.wait_ge(ps_ok, n + 1)
                act.activation(parts[0][:], ps, ACT.Copy).then_inc(high_ok, 1)

            def project_out(n, t, whole, parts, bias, e):
                act.wait_ge(qkv_ps[n], e.b + 1)
                if isinstance(e.b, int) and e.b == 0:
                    act.wait_ge(w_in["b" + n], 16)
                for c in range(NC):
                    last = act.activation(whole[:, c], chunks(t)[:, c], ACT.Identity, bias=bias[:, c:c + 1])
                last.then_inc(full[n], 1)
                for c in range(NC):
                    last = act.activation(parts[e.parity][:, 0, c], chunks(t)[:, c], ACT.Identity, bias=bias[:, c:c + 1])
                last.then_inc(part_h[n], 1)

            def middle_part(n, rest, parts, e):
                act.wait_ge(rest1[n], e.b + 1)
                act.activation(parts[e.parity][:, 1], rest[:], ACT.Copy).then_inc(part_m[n], 1)

            def softmax_head(s, h):
                g = h // HG
                if h % HG == 0 and g >= 2:
                    act.wait_ge(av_done, NG * s.b + g - 1)
                act.wait_ge(sc_ps, H * s.b + h + 1)
                act.activation(probs[g % 2][:, h % HG], chunks(2 + h % 2), ACT.Exp, scale=SCALE).then_inc(exp_done, 1)

            def copy_attention(s, half):
                act.wait_ge(av_done, NG * s.b + 2 * half + 2)
                act.activation(att_raw[:, 2 * half:2 * half + 2], chunks(4), ACT.Copy).then_inc(av_evac, 1)

            def post_exp(p):
                act.wait_ge(xs_neg, p.b + 1)
                for t in range(NT):
                    last = act.activation(xp[:, t], xsc[:, t], ACT.Exp, bias=xneg[:, t:t + 1], accum_out=xsum[:, t:t + 1])
                last.then_inc(xs_exp, 1)

            def post_up(p, t):
                act.wait_ge(up_ps, p.b + 1)
                act.activation(upT[:], chunks(t), ACT.Relu).then_inc(up_ok, 1)

            def post_xpT(p, t):
                act.wait_ge(xpT_ps, p.b + 1)
                act.activation(xpT[:], bank[t][0:SC, 0:S], ACT.Copy).then_inc(xpT_ok, 1)

            def heads(post, late, mid, early):
                if early and not late:
                    if early.b == 0:
                        for n in ("wq", "wv"):
                            weight_high(n)
                    for n, t, whole, rest, parts, bias in (("k", 7, kf, kr, kp, bk), ("q", 5, qf, qr, qp, bq)):
                        wait(act, rest1[n], early.b)
                        project_out(n, t, whole, parts, bias, early)
                    middle_part("k", kr, kp, early)
                    middle_part("q", qr, qp, early)
                    if early.b == 1:
                        for n in ("uw", "wo"):
                            weight_high(n)
                for h in range(H):
                    if late and not post and h in (3, 7):
                        weight_high({3: "u1", 7: "v1"}[h])
                    if late:
                        softmax_head(late, h)
                        if h == 12:
                            copy_attention(late, 0)
                    if early and late:
                        if h == 3:
                            project_out("q", 5, qf, qp, bq, early)
                        if h == 6:
                            middle_part("q", qr, qp, early)
                        if h == 8:
                            project_out("k", 7, kf, kp, bk, early)
                    if post:
                        if h == 4:
                            high_part(chunks(6), x1T, x1T_ps, x1T_h, post.b)
                        if h == 7:
                            post_up(post, 6)
                        if h == 10:
                            post_exp(post)
                        if h == 12:
                            post_xpT(post, 5)

            def between(post, late, mid, early):
                if post:
                    copy_attention(post, 1)
                if late:
                    act.wait_ge(mT_ps, late.b + 1)
                    act.activation(smax_T[:], bank[5][0:3 * H, 0:S // 2].bitcast(BF16), ACT.Copy).then_inc(mT_ok, 1)
                    act.wait_ge(mT_ok, late.b + 1)
                    act.dma_start(qs[late.parity][KR:KM], smax_T[:]).then_inc(mstacked[late.parity], 16)
                if post:
                    high_part(chunks(5), attT, attT_ps, attT_h, post.b)
                if early:
                    if isinstance(early.b, int) and early.b == 0:
                        weight_high("wk")
                    high_part(chunks(6), xT, xT_ps, xT_h, early.b)
                if late and not mid:
                    ffn_turned(0, (0, 1))

            def ffn_turned(i, banks):
                for c in range(NC):
                    act.wait_ge(x2T_ps, NC * i + c + 1)
                    act.activation(x2T[0][:, c], bank[banks[c]][:, :], ACT.Copy).then_inc(x2T_h, 1)

            def ffn(i, post):
                for f in range(NF):
                    act.wait_ge(hid_ps, NF * i + f + 1)
                    wait(act, gel_used, NF // 2 * i + (f - 4) // 2 + 1)
                    act.activation(gel[f % 4][:], bank[f % 2][:, :], ACT.Gelu_apprx_tanh, bias=b1[:, f:f + 1]).then_inc(gel_ok, 1)
                    if i + 1 < PAIRS and f == 1:
                        ffn_turned(i + 1, (6, 7))
                    if post and f == 5:
                        high_part(chunks(2), x1T, x1T_ps, x1T_h, post.b)
                        post_up(post, 2)
                if post:
                    post_exp(post)
                    post_xpT(post, 7)

            steps(act, between, heads)
            act.wait_ge(w_in["ffn"], 16 * LOADS["ffn"])
            for i in range(PAIRS):
                ffn(i, batch_at(0, B - 1) if i == 0 else None)

        @block.tensor
        def _(pe):
            pe.wait_ge(ident_ok, 4)
            parts_of = {n: (h, l) for n, (_, h, l) in weights.items()}

            def products(out, left, right, first=True, last=True):
                terms = ((0, 0), (0, 1), (1, 0))
                for n, (i, j) in enumerate(terms):
                    mm = pe.matmul(out, left[i], right[j], start=first and n == 0, stop=last and n == len(terms) - 1)
                return mm

            def to_channels(t, x, tiles):
                for c in range(NC):
                    for k in range(tiles):
                        last = pe.transpose(bank[t][:, c * S + k * P:c * S + (k + 1) * P], x[:, k, c * P:(c + 1) * P], ident[:])
                return last

            def project_rows(t, name, x):
                w = parts_of[name]
                for m in range(NC):
                    for c in range(NC):
                        last = products(chunks(t)[:, m], [w[i][:, c, m * P:(m + 1) * P] for i in range(2)], [x[i][:, c] for i in range(2)], c == 0, c == NC - 1)
                return last

            def project_tokens(t, name, x, tiles=range(NT)):
                w = parts_of[name]
                for k in tiles:
                    for c in range(NC):
                        last = products(chunks(t)[:, k], [x[i][:, c, k * P:(k + 1) * P] for i in range(2)], [w[i][:, c] for i in range(2)], c == 0, c == NC - 1)
                return last

            def max_scores(m, h):
                if h == 0:
                    if isinstance(m.b, int) and m.b < 2:
                        pe.wait_ge(stacked[m.parity][1], 2 * NP * 16)
                    else:
                        pe.wait_ge(stacked[m.parity][0], 2 * NP * 16 * m.turn)
                if h == HC:
                    pe.wait_ge(stacked[m.parity][1], 2 * NP * 16 * (m.turn + 1))
                if h >= 2:
                    pe.wait_ge(max_read, H * m.b + h - 1)
                for t in range(NT):
                    last = pe.matmul(chunks(h % 2)[:, t], qs[m.parity][0:KR, place(h), t * P:(t + 1) * P], ks[m.parity][0:KR, place(h)], start=True, stop=True)
                last.then_inc(max_ps, 1)

            def scores(s, h):
                if h == 0:
                    pe.wait_ge(mstacked[s.parity], 16 * (s.turn + 1))
                if h >= 2:
                    pe.wait_ge(exp_done, H * s.b + h - 1)
                for t in range(NT):
                    last = pe.matmul(chunks(2 + h % 2)[:, t], ks[s.parity][0:KM, place(h), t * P:(t + 1) * P], qs[s.parity][0:KM, place(h)], start=True, stop=True)
                last.then_inc(sc_ps, 1)

            def attend(s, g, post):
                if g == 0 and post:
                    pe.wait_ge(x1_ok, post.b + 1)
                if g == 2:
                    pe.wait_ge(av_evac, 2 * s.b + 1)
                pe.wait_ge(exp_done, H * s.b + HG * (g + 1))
                for t in range(NT):
                    for j in range(HG):
                        last = pe.matmul(chunks(4)[j * W:(j + 1) * W, g % 2], vsb[s.parity][:, t, HG * g + j], probs[g % 2][:, j, t],
                                         start=t == 0, stop=t == NT - 1, tile_position=(0, j * W))
                last.then_inc(av_done, 1)

            def post_x1T(p, t):
                pe.wait_ge(ln_done[1], p.b + 1)
                to_channels(t, x1n, NT).then_inc(x1T_ps, 1)

            def post_up(p, t):
                pe.wait_ge(x1T_l, p.b + 1)
                project_rows(t, "uw", x1T).then_inc(up_ps, 1)

            def post_xs(p, b):
                pe.wait_ge(uq_ok, p.b + 1)
                pe.wait_ge(up_ok, p.b + 1)
                for t in range(NT):
                    for c in range(NC):
                        last = pe.matmul(bank[b][:, t * SC:(t + 1) * SC], upT[:, c, t * P:(t + 1) * P], uqT[:, c], start=c == 0, stop=c == NC - 1)
                last.then_inc(xs_ps, 1)

            def post_xpT(p, b):
                pe.wait_ge(xs_exp, p.b + 1)
                for t in range(NT):
                    last = pe.transpose(bank[b][0:SC, t * P:(t + 1) * P], xp[:, t], ident[:])
                last.then_inc(xpT_ps, 1)

            def post_pv(p, b):
                pe.wait_ge(xpT_ok, p.b + 1)
                for t in range(NT):
                    last = pe.matmul(chunks(b)[:, t], xpT[:, t * P:(t + 1) * P], cbuf[p.parity][:], start=True, stop=True)
                last.then_inc(pv_ps, 1)

            def heads(post, late, mid, early):
                if early and not late:
                    pe.wait_ge(xT_l, early.b + 1)
                    for k, (n, t) in enumerate((("k", 7), ("q", 5))):
                        wait(pe, part_h[n], early.b)
                        if early.b == 0:
                            pe.wait_ge(w_low, k + 1)
                        project_rows(t, "w" + n, xT).then_inc(qkv_ps[n], 1)
                if mid and not late:
                    for h in range(2):
                        max_scores(mid, h)
                for h in range(H):
                    if mid and 1 <= h < H - 1:
                        max_scores(mid, h + 1)
                    if late and 1 <= h < H - 1:
                        scores(late, h + 1)
                    if early and late and h == 2:
                        pe.wait_ge(xT_l, early.b + 1)
                        if not post:
                            pe.wait_ge(mT_ok, late.b + 1)
                            pe.wait_ge(part_h["k"], early.b)
                        project_rows(5, "wq", xT).then_inc(qkv_ps["q"], 1)
                    if late and h % HG == 1 and h > HG:
                        attend(late, h // HG - 1, post)
                    if early and late and h == 6:
                        if post:
                            pe.wait_ge(uq_ok, post.b + 1)
                        project_rows(7, "wk", xT).then_inc(qkv_ps["k"], 1)
                    if post:
                        if h == 4:
                            post_x1T(post, 6)
                        if h == 6:
                            post_up(post, 6)
                        if h == 8:
                            post_xs(post, 6)
                        if h == 12:
                            if early:
                                pe.wait_ge(part_h["q"], early.b + 1)
                            elif not mid:
                                pe.wait_ge(low_ok, 1)
                            post_xpT(post, 5)
                        if h == 14:
                            if early:
                                pe.wait_ge(part_h["k"], early.b + 1)
                            post_pv(post, 7)
                    if late and not mid and h == 1:
                        low_rank(0)

            def between(post, late, mid, early):
                def values(tiles):
                    return project_tokens(6, "wv", xT, tiles)

                if mid:
                    if isinstance(mid.b, int) and mid.b == 0:
                        pe.wait_ge(w_low, 3)
                    values([0])
                if post:
                    n = post.b
                    attend(post, NG - 1, None)
                if mid:
                    values([1]).then_inc(qkv_ps["v"], 1)
                if late:
                    pe.wait_ge(mparts, late.b + 1)
                    if mid:
                        pe.wait_ge(part_h["q"], mid.b + 1)
                    for t in range(NT):
                        last = pe.transpose(bank[5][0:5 * H, t * P // 2:(t + 1) * P // 2].bitcast(BF16),
                                            smax_p[:, t].rearrange("p k h -> p (k h)"), ident_bf[:])
                    last.then_inc(mT_ps, 1)
                if post:
                    pe.wait_ge(c_in[post.parity], 16 * (post.turn + 1))
                    if mid:
                        pe.wait_ge(part_h["k"], mid.b + 1)
                    if not late:
                        pe.wait_ge(x2_ok, n)
                    for c in range(NC):
                        last = pe.transpose(bank[7][:, c * SC:(c + 1) * SC], cbuf[post.parity][:, c * P:(c + 1) * P], ident[0:SC, 0:SC])
                    last.then_inc(cT_ps, 1)
                    pe.wait_ge(av_evac, 2 * n + 2)
                    for t in range(NT):
                        for g in range(NG):
                            last = pe.transpose(bank[2 + t][:, g * P:(g + 1) * P], att_raw[:, g, t * P:(t + 1) * P], ident[:])
                        last.then_inc(att_ps, 1)
                    pe.wait_ge(cT_ok, n + 1)
                    for m in range(NC):
                        for c in range(NC):
                            last = pe.matmul(bank[7][:, 256 + m * SC:256 + (m + 1) * SC], weights["uw"][0][:, c, m * P:(m + 1) * P], cT[:, c],
                                             start=c == 0, stop=c == NC - 1)
                    last.then_inc(uq_ps, 1)
                if mid and late:
                    for h in range(2):
                        max_scores(mid, h)
                if post:
                    pe.wait_ge(att_ok, NT * (n + 1))
                    if late:
                        pe.wait_ge(mT_ok, late.b + 1)
                    to_channels(5, att, NT).then_inc(attT_ps, 1)
                if early:
                    pe.wait_ge(ln_done[0], early.b + 1)
                    if mid:
                        pe.wait_ge(v_ok, mid.b + 1)
                    to_channels(6, xn, NT).then_inc(xT_ps, 1)
                if late:
                    if isinstance(late.b, int) and late.b == 0:
                        pe.wait_ge(const_ok, 4)
                        pe.wait_ge(v_zero, 5)
                    for h in range(2):
                        scores(late, h)
                if post:
                    if isinstance(n, int) and n == 0:
                        pe.wait_ge(w_low_later, 2)
                    if late and not mid:
                        ffn_turn(0, (0, 1))
                    if not late:
                        hidden(0, 0)
                        hidden(0, 1)
                    pe.wait_ge(attT_l, n + 1)
                    project_tokens(4, "wo", attT).then_inc(proj_ps, 1)

            def ffn_turn(i, banks):
                pe.wait_ge(ln_done[2], i + 1)
                for c in range(NC):
                    for t in range(FT):
                        last = pe.transpose(bank[banks[c]][:, t * P:(t + 1) * P], x2n[:, t, c * P:(c + 1) * P], ident[:])
                    last.then_inc(x2T_ps, 1)

            def low_rank(i):
                pe.wait_ge(x2T_l, NC * (i + 1))
                if i == 0:
                    pe.wait_ge(w_low_later, 4)
                u1 = parts_of["u1"]
                for c in range(NC):
                    last = products(bank[5][:, :], [u1[k][:, c] for k in range(2)], [x2T[k][:, c] for k in range(2)], c == 0, c == NC - 1)
                last.then_inc(low_ps, 1)

            def hidden(i, f):
                if f == 0:
                    pe.wait_ge(low_ok, i + 1)
                wait(pe, gel_ok, NF * i + f - 1)
                for k in range(2):
                    last = pe.matmul(bank[f % 2][:, :], parts_of["v1"][k][:, f * P:(f + 1) * P], low[:], start=k == 0, stop=k == 1)
                last.then_inc(hid_ps, 1)

            def rank(i, f):
                pe.wait_ge(gel_ok, NF * i + f + 2)
                for k in range(2):
                    last = pe.matmul(bank[3][k * R:(k + 1) * R, :], u2[:, f + k], gel[(f + k) % 4][:], start=f == 0, stop=f == NF - 2,
                                     tile_position=(0, k * R))
                last.then_inc(gel_used, 1)

            def ffn(i, post):
                if post:
                    pe.wait_ge(uq_ok, post.b + 1)
                if i + 1 < PAIRS:
                    ffn_turn(i + 1, (6, 7))
                for f in range(0, NF, 2):
                    if f + 2 < NF:
                        hidden(i, f + 2)
                        hidden(i, f + 3)
                    if post and f == 4:
                        post_xs(post, 2)
                    rank(i, f)
                    if f == 2:
                        if post:
                            post_x1T(post, 2)
                        if i + 1 < PAIRS:
                            low_rank(i + 1)
                        if post:
                            post_up(post, 2)
                if i + 1 < PAIRS:
                    hidden(i + 1, 0)
                    hidden(i + 1, 1)
                pe.wait_ge(r2_ok, i + 1)
                for half in range(2):
                    if post and half == 1:
                        post_xpT(post, 7)
                    for t in range(NT):
                        k = half * NT + t
                        last = pe.matmul(chunks((4, 2)[half])[:, t], rank2[:, k * P:(k + 1) * P], v2[:], start=True, stop=True)
                    last.then_inc(out_ps, 1)
                if post:
                    post_pv(post, 5)

            steps(pe, between, heads)
            for i in range(PAIRS):
                ffn(i, batch_at(0, B - 1) if i == 0 else None)


INS = ("x", "ctx", "mask", "wq", "wk", "wv", "wo", "uw", "bq", "bk", "bv", "bo", "dpar", "u1", "v1", "b1", "u2", "v2", "b2")


def kernel(x, ctx_1024, mask_BxS2_bf0, mask_BxS2_bk1, L0_attn_Wq, L0_attn_bq, L0_attn_Wk, L0_attn_bk, L0_attn_Wv, L0_attn_bv,
           L0_attn_Wo, L0_attn_bo, L0_xattn_U_w, L0_xattn_D_param, L0_ffn_U1, L0_ffn_V1, L0_ffn_b1, L0_ffn_U2, L0_ffn_V2, L0_ffn_b2):
    import concourse.bacc as bacc
    from concourse.bass_utils import run_bass_kernel_spmd

    heads, D = 16, x.shape[-1]
    chunks, dh = D // P, D // heads

    def head_minor(w):
        w = np.asarray(w)
        w4 = w.reshape(chunks, heads // chunks, dh, *w.shape[1:])
        return np.transpose(w4, (0, 2, 1, *range(3, w4.ndim))).reshape(w.shape)

    def columns(v):
        return np.asarray(v).reshape(-1, P).T

    laid = {
        "x": x, "ctx": ctx_1024, "mask": mask_BxS2_bk1,
        "wq": head_minor(L0_attn_Wq).T, "wk": head_minor(L0_attn_Wk).T, "wv": np.asarray(L0_attn_Wv).T, "wo": np.asarray(L0_attn_Wo).T,
        "uw": np.asarray(L0_xattn_U_w).T, "bq": columns(head_minor(L0_attn_bq)), "bk": columns(head_minor(L0_attn_bk)),
        "bv": L0_attn_bv, "bo": L0_attn_bo, "dpar": columns(L0_xattn_D_param), "u1": L0_ffn_U1, "v1": L0_ffn_V1,
        "b1": columns(L0_ffn_b1), "u2": L0_ffn_U2, "v2": L0_ffn_V2, "b2": L0_ffn_b2,
    }
    nc = bacc.Bacc("TRN2", target_bir_lowering=False, num_devices=1)
    arrays, io = {}, {}
    for name in INS:
        a = np.ascontiguousarray(laid[name])
        arrays[f"in_{name}"] = a
        io[name] = nc.dram_tensor(f"in_{name}", a.shape, mybir.dt.from_np(a.dtype), kind="ExternalInput").ap()
    io["out"] = nc.dram_tensor("out_y", x.shape, F32, kind="ExternalOutput").ap()
    decoder_layer(nc, io)
    return run_bass_kernel_spmd(nc, [arrays], core_ids=[0]).results[0]["out_y"]
```
